# Optimizing a Trainium2 kernel written in Bass

```python
import numpy as np
import jax
import jax.numpy as jnp

def _softmax(x, axis=-1):
    return jax.nn.softmax(x, axis=axis)

def _gelu(x):
    return jax.nn.gelu(x, approximate=True)

def _silu(x):
    return jax.nn.silu(x)

def _sigmoid(x):
    return jax.nn.sigmoid(x)

def _layernorm(x, axis=-1, eps=1e-05):
    m = jnp.mean(x, axis=axis, keepdims=True)
    v = jnp.var(x, axis=axis, keepdims=True)
    return (x - m) / jnp.sqrt(v + eps)

def _scatter_add(tgt, idx, src, axis=0):
    return tgt.at[idx].add(src)

def _segment_sum(src, seg, n):
    return jax.ops.segment_sum(src, seg, n)
kernel_name = 'mk_seq_preln_d1_jaxref_r8_8239ca'

def setup_inputs(seed: int=0):
    np.random.seed(seed)
    _w = jnp.asarray

    def _L0_attn_setup():
        import jax, jax.numpy as jnp
        import numpy as np
        INFTY_APPROX = 1e+30
        ROTARY_BASE = 10000.0
        D_HEAD = 128

        def rope(x):
            *_, length, width = x.shape
            half = width // 2
            positions = jnp.arange(length)[:, None].astype(x.dtype)
            dims = jnp.arange(half).astype(x.dtype)
            ang_freqs = jnp.power(ROTARY_BASE, -dims / half)[None, :]
            radians = positions * ang_freqs
            cos = jnp.cos(radians)[None, None].astype(x.dtype)
            sin = jnp.sin(radians)[None, None].astype(x.dtype)
            even, odd = jnp.split(x, 2, axis=-1)
            r_even = even * cos - odd * sin
            r_odd = even * sin + odd * cos
            return jnp.concatenate([r_even, r_odd], axis=-1)
        key = jax.random.key(seed)
        ks = jax.random.split(key, 5)
        B, T, M, D = (4, 256, 128, D_HEAD)
        H = M // D
        x = jax.random.normal(ks[0], (B, T, M), dtype=jnp.float32)
        scale = M ** (-0.5)
        wq = jax.random.normal(ks[1], (H, M, D), dtype=jnp.float32) * scale
        wk = jax.random.normal(ks[2], (H, M, D), dtype=jnp.float32) * scale
        wv = jax.random.normal(ks[3], (H, M, D), dtype=jnp.float32) * scale
        wo = jax.random.normal(ks[4], (H, D, M), dtype=jnp.float32) * scale
        return {'x': x, 'wq': wq, 'wk': wk, 'wv': wv, 'wo': wo}
    _L0_attn_in = _L0_attn_setup()

    def _L0_ffn_setup():
        import jax, jax.numpy as jnp
        import numpy as np
        B, SEQ, D, E, F = (4, 128, 128, 8, 512)
        CAPACITY = 2
        key = jax.random.key(seed)
        ks = jax.random.split(key, 8)
        x = jax.random.normal(ks[0], (B, SEQ, D), jnp.float32)
        gate_weight = jax.random.normal(ks[1], (E, D), jnp.float32) * 0.006
        W1 = jax.random.normal(ks[2], (E, D, F), jnp.float32) * (1.0 / np.sqrt(D))
        b1 = jnp.zeros((E, F), jnp.float32)
        W2 = jax.random.normal(ks[3], (E, F, D), jnp.float32) * (1.0 / np.sqrt(F))
        b2 = jnp.zeros((E, D), jnp.float32)
        Ws1 = jax.random.normal(ks[4], (D, F), jnp.float32) * (1.0 / np.sqrt(D))
        bs1 = jnp.zeros((F,), jnp.float32)
        Ws2 = jax.random.normal(ks[5], (F, D), jnp.float32) * (1.0 / np.sqrt(F))
        bs2 = jnp.zeros((D,), jnp.float32)
        return {'x': x, 'gate_weight': gate_weight, 'W1': W1, 'b1': b1, 'W2': W2, 'b2': b2, 'Ws1': Ws1, 'bs1': bs1, 'Ws2': Ws2, 'bs2': bs2}
    _L0_ffn_in = _L0_ffn_setup()
    _d = {'L0_attn_x': _L0_attn_in['x'], 'L0_attn_wq': _L0_attn_in['wq'], 'L0_attn_wk': _L0_attn_in['wk'], 'L0_attn_wv': _L0_attn_in['wv'], 'L0_attn_wo': _L0_attn_in['wo'], 'L0_ffn_gate_weight': _L0_ffn_in['gate_weight'], 'L0_ffn_W1': _L0_ffn_in['W1'], 'L0_ffn_b1': _L0_ffn_in['b1'], 'L0_ffn_W2': _L0_ffn_in['W2'], 'L0_ffn_b2': _L0_ffn_in['b2'], 'L0_ffn_Ws1': _L0_ffn_in['Ws1'], 'L0_ffn_bs1': _L0_ffn_in['bs1'], 'L0_ffn_Ws2': _L0_ffn_in['Ws2'], 'L0_ffn_bs2': _L0_ffn_in['bs2']}
    _x0 = _d['L0_attn_x']
    _d['L0_attn_x'] = jax.random.normal(jax.random.fold_in(jax.random.key(seed), 1), (4, 1024, 128), dtype=_x0.dtype)
    del _x0
    return _d

def reference(L0_attn_x, L0_attn_wq, L0_attn_wk, L0_attn_wv, L0_attn_wo, L0_ffn_gate_weight, L0_ffn_W1, L0_ffn_b1, L0_ffn_W2, L0_ffn_b2, L0_ffn_Ws1, L0_ffn_bs1, L0_ffn_Ws2, L0_ffn_bs2):

    def _L0_attn_ref(x, wq, wk, wv, wo):
        import jax, jax.numpy as jnp
        import numpy as np
        INFTY_APPROX = 1e+30
        ROTARY_BASE = 10000.0
        D_HEAD = 128

        def rope(x):
            *_, length, width = x.shape
            half = width // 2
            positions = jnp.arange(length)[:, None].astype(x.dtype)
            dims = jnp.arange(half).astype(x.dtype)
            ang_freqs = jnp.power(ROTARY_BASE, -dims / half)[None, :]
            radians = positions * ang_freqs
            cos = jnp.cos(radians)[None, None].astype(x.dtype)
            sin = jnp.sin(radians)[None, None].astype(x.dtype)
            even, odd = jnp.split(x, 2, axis=-1)
            r_even = even * cos - odd * sin
            r_odd = even * sin + odd * cos
            return jnp.concatenate([r_even, r_odd], axis=-1)
        q = jnp.einsum('bim,hmd->bhid', x, wq)
        k = jnp.einsum('bim,hmd->bhid', x, wk)
        v = jnp.einsum('bim,hmd->bhid', x, wv)
        q = rope(q)
        k = rope(k)
        mult = jnp.asarray(D_HEAD ** (-0.5), dtype=x.dtype)
        s = jnp.einsum('bhid,bhjd->bhij', q * mult, k * mult)
        T = s.shape[-1]
        i = jnp.arange(T)[:, None]
        j = jnp.arange(T)[None, :]
        mask = (i < j).astype(s.dtype)[None, None]
        s = s - jnp.asarray(INFTY_APPROX, dtype=s.dtype) * mask
        p = jax.nn.softmax(s, axis=-1)
        o = jnp.einsum('bhij,bhjd->bhid', p, v)
        r = jnp.einsum('bhid,hdm->bim', o, wo)
        return r

    def _L0_ffn_ref(x, gate_weight, W1, b1, W2, b2, Ws1, bs1, Ws2, bs2):
        import jax, jax.numpy as jnp
        import numpy as np
        B, SEQ, D, E, F = (4, 128, 128, 8, 512)
        CAPACITY = 2
        Bb, s, Dd = x.shape
        Ee = gate_weight.shape[0]
        xf = x.reshape(-1, Dd)
        S = xf.shape[0]
        logits = xf @ gate_weight.T
        scores = jax.nn.softmax(logits, axis=-1).T
        k = S * CAPACITY
        vals, idx = jax.lax.top_k(scores.reshape(-1), k)
        eidx = idx // S
        tidx = idx % S
        gate = jnp.zeros((Ee, S), x.dtype).at[eidx, tidx].add(vals)
        h = jax.nn.gelu(jnp.einsum('sd,edf->esf', xf, W1) + b1[:, None, :], approximate=True)
        y = jnp.einsum('esf,efd->esd', h, W2) + b2[:, None, :]
        out = jnp.einsum('es,esd->sd', gate, y)
        shared = jax.nn.gelu(xf @ Ws1 + bs1, approximate=True) @ Ws2 + bs2
        out = out + shared
        return out.reshape(Bb, s, Dd)
    x = L0_attn_x
    x = x + _L0_attn_ref(_layernorm(x, axis=-1), L0_attn_wq, L0_attn_wk, L0_attn_wv, L0_attn_wo)
    x = x + _L0_ffn_ref(_layernorm(x, axis=-1), L0_ffn_gate_weight, L0_ffn_W1, L0_ffn_b1, L0_ffn_W2, L0_ffn_b2, L0_ffn_Ws1, L0_ffn_bs1, L0_ffn_Ws2, L0_ffn_bs2)
    return x

_drawn_inputs = setup_inputs


def setup_inputs(seed=0):
    import zlib

    import numpy as np

    out = dict(_drawn_inputs(seed))
    spreads = {'L0_ffn_b1': (0.0, 0.754),
     'L0_ffn_b2': (0.0, 0.515),
     'L0_ffn_bs1': (0.0, 0.1),
     'L0_ffn_bs2': (0.0, 0.1)}
    factors = {'L0_attn_wq': 5.235, 'L0_attn_wk': 4.879}
    for name, (base, spread) in spreads.items():
        noise = np.random.default_rng([zlib.crc32(name.encode()), seed]).standard_normal(out[name].shape)
        drawn = base * np.exp(spread * noise) if base else spread * noise
        out[name] = jnp.asarray(drawn.astype(out[name].dtype))
    for name, factor in factors.items():
        out[name] = (out[name] * factor).astype(out[name].dtype)
    return out
```

```python
from contextlib import ExitStack

import concourse.bass as bass
from concourse import mybir

ALU = mybir.AluOpType
ACT = mybir.ActivationFunctionType
AX = mybir.AxisListType
F32 = mybir.dt.float32
F32R = mybir.dt.float32r
BF16 = mybir.dt.bfloat16
I32 = mybir.dt.int32

P = 128
EPS = 1e-5
MASKED = -1e30
LOG2E = 1.4426950408889634
LN2_HI = 0.693359375
LN2_LO = -2.12194440e-4
ROUND = 12582912.0
RSQRT_MAGIC = 0x5F3759DF


def moe_layer(nc, x_in, wq_in, wk_in, wv_in, wo_in, gate_in, W1_in, b1_in, W2_in, b2_in,
              Ws1_in, bs1_in, Ws2_in, bs2_in, cos_in, sin_in, out):
    B, T, D = x_in.shape
    E, _, F = W1_in.shape
    assert D == P and F % P == 0 and T % 512 == 0
    TB = T // P
    NT = B * TB
    S = B * T
    NF = F // P
    K_TOP = 2 * S
    CH = 512
    NC = S // CH
    NE = E + 1
    QK_SCALE = 1.0 / D
    NBIT = 30
    assert NC == 8 and E % 2 == 0 and TB == 8 and NBIT == 5 * (NC - 2)

    RING = TB + 8
    R_XN, R_Q, R_QS, R_K, R_KS, R_V, R_S, R_XN2, R_LG = 0, 1, 2, 3, 4, 5, 6, 6 + TB, 7 + TB
    TURNS = sum((i + 4) // 4 for i in range(TB))

    ROWS_B1, ROWS_B2, ROWS_GW = 0, NE * NF, NE * NF + NE
    NROWS = ROWS_GW + E

    with ExitStack() as ctx:
        def sb(name, shape, dt):
            return ctx.enter_context(nc.sbuf_tensor(name, shape, dt))

        def pb(name, shape, dt):
            return ctx.enter_context(nc.psum_tensor(name, shape, dt))

        def sem(name):
            return ctx.enter_context(nc.semaphore(name))

        ident = sb("ident", [P, P], F32)
        ident_b = sb("ident_b", [P, P], BF16)
        mask_b = sb("mask_b", [P, P], BF16)
        before_b = sb("before_b", [P, P], BF16)
        ones_b = sb("ones_b", [P, P], BF16)
        pick_b = sb("pick_b", [P, E, P], BF16)
        costab = sb("costab", [P, T], F32)
        sintab = sb("sintab", [P, T], F32)
        w4 = sb("w4", [P, 4, D], F32)
        wvo = sb("wvo", [P, 3, D], F32)
        wp = sb("wp", [P, D], F32)
        rows = sb("rows", [NROWS, P], F32)
        cols = sb("cols", [P, NROWS], F32)
        gw_hi = sb("gw_hi", [P, P], F32R)
        gw_lo = sb("gw_lo", [P, P], F32R)
        x2 = sb("x2", [P, NT, D], F32)
        xn = sb("xn", [P, TB, D], F32)
        xnT = sb("xnT", [P, T], F32)
        q = sb("q", [P, T], F32)
        k = sb("k", [P, T], F32)
        qk_sin = sb("qk_sin", [P, T], F32)
        v = sb("v", [P, TB, D], F32)
        prob = sb("prob", [P, 2, T], F32)
        probT = sb("probT", [P, 2, TB, P], F32)
        neg_max = sb("neg_max", [P, TB], F32)
        row_sum = sb("row_sum", [P, TB], F32)
        row_inv = sb("row_inv", [P, TB], F32)
        stats = sb("stats", [P, TB, 6], F32)
        mv = sb("mv", [P, TB, 2], F32)
        nw = sb("nw", [P, 4, TB], F32)
        nwi = sb("nwi", [P, TB], I32)
        xT_hi = sb("xT_hi", [P, S], F32R)
        xT_lo = sb("xT_lo", [P, S], F32R)
        lg = sb("lg", [P, E, NT], F32)
        ra = sb("ra", [P, E, NT], F32)
        rb = sb("rb", [P, E, NT], F32)
        pow2 = sb("pow2", [P, E, NT], I32)
        rs = sb("rs", [P, 2, NT], F32)
        bit = sb("bit", [P, 32], I32)
        found = sb("found", [P, 1], I32)
        cand = sb("cand", [P, 1], I32)
        flag = sb("flag", [P, 1], I32)
        count_b = sb("count_b", [P, 1], BF16)
        count_f = sb("count_f", [P, 2], F32)
        eq_b = sb("eq_b", [P, E * NT], BF16)
        zeros = sb("zeros", [P, E * NT], F32)
        g_parts = sb("g_parts", [P, NT, 3, E], BF16)
        gT = sb("gT", [P, S], BF16)
        lgT = sb("lgT", [P, T], F32)
        w_raw = sb("w_raw", [P, 2, 2 * F], F32)
        w_hi = sb("w_hi", [P, 2, 2 * F], F32R)
        w_lo = sb("w_lo", [P, 2, 2 * F], F32R)
        h = [prob[:].rearrange("p a (f c) -> p (a f) c", c=CH), probT[:].rearrange("p a (f t) c -> p (a f) (t c)", f=2)]
        h_hi = sb("h_hi", [P, 2, NF, CH], F32R)
        h_lo = sb("h_lo", [P, 2, NF, CH], F32R)
        bias_now = sb("bias_now", [P, 2, NF], F32)
        gate_bc = sb("gate_bc", [P, 2, CH], F32)
        gated = sb("gated", [P, 2, CH], F32)
        outT = sb("outT", [P, S], F32)

        big = [pb(f"big{i}", [P, 1024], F32) for i in range(2)]
        turn = [pb(f"turn{i}", [P, 512], F32) for i in range(2)]
        summ = [pb(f"summ{i}", [P, 512], F32) for i in range(2)]
        hbank = [big[f // 2][:, (f % 2) * 512:(f % 2) * 512 + 512] for f in range(NF)]

        s_w = sem("attention_weights_loaded")
        s_x = sem("x_loaded")
        s_const = sem("constants_ready")
        s_pe0 = sem("setup_products_done")
        s_act0 = sem("setup_copies_done")
        s_xn = sem("normed_ready")
        s_big = sem("scores_slot_filled")
        s_xnT = sem("normed_turned")
        s_rot = sem("rotation_part_ready")
        s_qk = sem("query_or_key_ready")
        s_v = sem("values_ready")
        s_max = sem("row_max_ready")
        s_prob = sem("probs_ready")
        s_turn = sem("probs_turned")
        s_probT = sem("turned_probs_copied")
        s_att = sem("attention_tile_summed")
        s_x2 = sem("attention_added")
        s_hi2 = sem("normed2_hi_ready")
        s_lo2 = sem("normed2_lo_ready")
        s_lg = sem("logits_copied")
        s_lgT = sem("logits_turned")
        s_lgc = sem("logits_by_token_ready")
        s_gw = sem("gate_weight_ready")
        s_raw = sem("expert_weights_loaded")
        s_whi = sem("expert_weights_hi_ready")
        s_wlo = sem("expert_weights_lo_ready")
        s_bias = sem("expert_bias_copied")
        s_h = sem("hidden_chunk_summed")
        s_gelu = sem("gelu_chunk_ready")
        s_hp = sem("hidden_hi_ready")
        s_hilo = sem("hidden_split_ready")
        s_y = sem("expert_step_summed")
        s_gbank = sem("gate_rows_spread")
        s_gbc = sem("gate_rows_copied")
        s_gated = sem("expert_step_gated")
        s_acc = sem("expert_step_added")
        s_cnt = sem("count_ready")
        s_tot = sem("count_summed")
        s_gp = sem("gate_parts_ready")
        s_gt = sem("gate_parts_turned")
        s_gTc = sem("gate_parts_copied")
        s_fin = sem("result_turned")
        s_res = sem("result_added")
        s_out = sem("result_stored")
        s_dve = sem("vector_chain")
        s_pool0 = sem("pool_chain")

        block = ctx.enter_context(nc.Block())

        @block.sync
        def _(sp):
            def load_batch(b):
                sp.dma_start(x2[:, bass.ds(b * TB, TB), :],
                             x_in[bass.ds(b, 1), :, :].rearrange("a (t p) d -> p (a t) d", p=P)).then_inc(s_x, 16)

            load_batch(0)
            with nc.sync.Fori(1, B) as b:
                sp.wait_ge(s_x, b * 16)
                load_batch(b)

            def load_expert(par, w1, w2):
                sp.dma_start(w_raw[:, par, 0:F], w1).then_inc(s_raw, 16)
                sp.dma_start(w_raw[:, par, F:2 * F].rearrange("p (c d) -> p c d", d=D), w2).then_inc(s_raw, 16)

            def w1_of(e):
                return W1_in[bass.ds(e, 1), :, :].rearrange("a d f -> d (a f)")

            def w2_of(e):
                return W2_in[bass.ds(e, 1), :, :].rearrange("a (c p) d -> p (a c) d", p=P)

            load_expert(0, Ws1_in, Ws2_in.rearrange("(c p) d -> p c d", p=P))
            sp.wait_ge(s_raw, 32)
            load_expert(1, w1_of(0), w2_of(0))
            with nc.sync.Fori(0, E // 2 - 1) as ep:
                for par in range(2):
                    sp.wait_ge(s_wlo, ep * 2 + (par + 2))
                    load_expert(par, w1_of(ep * 2 + (par + 1)), w2_of(ep * 2 + (par + 1)))
            sp.wait_ge(s_wlo, E)
            load_expert(0, w1_of(E - 1), w2_of(E - 1))
            for b in range(B):
                sp.wait_ge(s_res, b + 1)
                sp.dma_start(out[b, :, :].rearrange("(t p) d -> p t d", p=P),
                             x2[:, b * TB:(b + 1) * TB, :]).then_inc(s_out, 16)
            sp.wait_ge(s_out, 16 * B)

        @block.gpsimd
        def _(pool):
            g = nc.gpsimd
            n = [0]

            def then(ins):
                n[0] += 1
                ins.then_inc(s_pool0, 1)
                pool.wait_ge(s_pool0, n[0])

            then(g.memset(ident[:], 0.0))
            then(g.affine_select(out=ident[:], in_=ident[:], compare_op=ALU.not_equal, fill=1.0, base=0,
                                 pattern=[[-1, P]], channel_multiplier=1))
            g.tensor_copy(ident_b[:], ident[:]).then_inc(s_const, 1)
            then(g.memset(mask_b[:], 0.0))
            g.affine_select(out=mask_b[:], in_=mask_b[:], compare_op=ALU.is_ge, fill=MASKED, base=0,
                            pattern=[[-1, P]], channel_multiplier=1).then_inc(s_const, 1)
            g.memset(ones_b[:], 1.0).then_inc(s_const, 1)
            then(g.memset(before_b[:], 0.0))
            g.affine_select(out=before_b[:], in_=before_b[:], compare_op=ALU.is_ge, fill=1.0, base=0,
                            pattern=[[-1, P]], channel_multiplier=1).then_inc(s_const, 1)
            then(g.memset(pick_b[:], 0.0))
            for part in range(3):
                then(g.affine_select(out=pick_b[:], in_=pick_b[:], compare_op=ALU.not_equal, fill=1.0,
                                     base=-part * E, pattern=[[-1, E], [0, P]], channel_multiplier=1))
            g.memset(gw_hi[:].bitcast(F32), 0.0).then_inc(s_const, 1)
            g.memset(gw_lo[:].bitcast(F32), 0.0).then_inc(s_const, 1)
            g.memset(gT[:].bitcast(F32), 0.0).then_inc(s_const, 1)
            g.memset(gate_bc[:, 1, :], 1.0).then_inc(s_const, 1)
            g.memset(zeros[:], 0.0).then_inc(s_const, 1)
            for half in range(2):
                g.memset(outT[:, half * (S // 2):(half + 1) * (S // 2)], 0.0).then_inc(s_acc, 1)

            with nc.gpsimd.Fori(0, B) as b:
                for j, t in enumerate((q, k)):
                    pool.wait_ge(s_rot, b * 4 + (2 * j + 2))
                    g.tensor_tensor(t[:], t[:], qk_sin[:], ALU.add).then_inc(s_qk, 1)

            def split_weights(par, n_whi):
                pool.wait_ge(s_whi, n_whi)
                g.tensor_tensor(w_lo[:, par, :], w_raw[:, par, :], w_hi[:, par, :].bitcast(F32),
                                ALU.subtract).then_inc(s_wlo, 1)

            def accumulate(done, c, par):
                pool.wait_ge(s_gated, done + 1)
                o = outT[:, bass.ds(c * CH, CH)]
                g.tensor_tensor(o, o, gated[:, par, :], ALU.add).then_inc(s_acc, 1)

            split_weights(0, 1)
            split_weights(1, 2)
            pool.wait_ge(s_acc, 2)
            with nc.gpsimd.Fori(0, NC // 2) as cp:
                for j in range(2):
                    accumulate(cp * 2 + j, cp * 2 + j, j)

            def expert(e, par, split):
                for j in range(2):
                    accumulate(e * NC + j, j, j)
                if split:
                    split_weights(1 - par, e + 2)
                with nc.gpsimd.Fori(1, NC // 2) as cp:
                    for j in range(2):
                        accumulate(e * NC + (cp * 2 + j), cp * 2 + j, j)

            with nc.gpsimd.Fori(0, E // 2 - 1) as ep:
                expert(ep * 2 + 1, 1, True)
                expert(ep * 2 + 2, 0, True)
            expert(E - 1, 1, True)
            expert(E, 0, False)

        @block.scalar
        def _(act):
            a = nc.scalar
            H = D // 2
            for j, w in ((0, wq_in), (2, wk_in)):
                w = w.rearrange("h m d -> m (h d)")
                act.dma_start(w4[:, j, :], w).then_inc(s_w, 16)
                act.dma_start(w4[:, j + 1, 0:H], w[:, H:D]).then_inc(s_w, 16)
                act.dma_start(w4[:, j + 1, H:D], w[:, 0:H]).then_inc(s_w, 16)
            act.dma_start(wvo[:, 0, :], wv_in.rearrange("h m d -> m (h d)")).then_inc(s_w, 16)
            act.dma_start(wvo[:, 2, :], wo_in.rearrange("h d m -> d (h m)")).then_inc(s_w, 16)
            act.dma_start(rows[ROWS_B1:ROWS_B1 + NF, :], bs1_in.rearrange("(c p) -> c p", p=P)).then_inc(s_w, 16)
            act.dma_start(rows[ROWS_B1 + NF:ROWS_B2, :], b1_in.rearrange("e (c p) -> (e c) p", p=P)).then_inc(s_w, 16)
            act.dma_start(rows[ROWS_B2:ROWS_B2 + 1, :], bs2_in.rearrange("(a p) -> a p", a=1)).then_inc(s_w, 16)
            act.dma_start(rows[ROWS_B2 + 1:ROWS_GW, :], b2_in).then_inc(s_w, 16)
            act.dma_start(rows[ROWS_GW:NROWS, :], gate_in).then_inc(s_w, 16)
            act.dma_start(costab[:], cos_in).then_inc(s_w, 16)
            act.dma_start(sintab[:], sin_in).then_inc(s_w, 16)
            act.wait_ge(s_w, 15 * 16)
            a.mul(w4[:, 0:2, :], w4[:, 0:2, :], QK_SCALE).then_inc(s_act0, 1)
            act.wait_ge(s_pe0, 1)
            a.copy(wvo[:, 1, :], turn[0][:, 0:P]).then_inc(s_act0, 1)
            act.wait_ge(s_pe0, 2)
            a.copy(cols[:], turn[1][:, 0:NROWS]).then_inc(s_act0, 1)
            act.wait_ge(s_act0, 3)
            act.wait_ge(s_const, 6)
            a.copy(gw_hi[:, 0:E], cols[:, ROWS_GW:NROWS]).then_inc(s_act0, 1)
            act.wait_ge(s_pe0, 3)
            a.copy(wp[:], turn[0][:, 0:P]).then_inc(s_act0, 1)

            def split_weights(par, n_raw):
                act.wait_ge(s_raw, n_raw)
                a.copy(w_hi[:, par, :], w_raw[:, par, :]).then_inc(s_whi, 1)

            with nc.scalar.Fori(0, B) as b:
                act.wait_ge(s_big, b * RING + (R_XN + 1))
                a.copy(xnT[:], big[R_XN % 2][:]).then_inc(s_xnT, 1)
                act.wait_ge(s_big, b * RING + (R_V + 1))
                a.copy(v[:].rearrange("p t d -> p (t d)"), big[R_V % 2][:]).then_inc(s_v, 1)
                used = 0
                for i in range(TB + 1):
                    if i < TB:
                        n = (i + 1) * P
                        act.wait_ge(s_max, b * TB + (i + 1))
                        a.activation(prob[:, i % 2, 0:n], big[(R_S + i) % 2][:, 0:n], ACT.Exp,
                                     bias=neg_max[:, i:i + 1],
                                     accum_out=row_sum[:, i:i + 1]).then_inc(s_prob, 1)
                    if i:
                        j = i - 1
                        if j >= 2:
                            act.wait_ge(s_att, b * TB + (j - 1))
                        for lo in range(0, j + 1, 4):
                            m = min(4, j + 1 - lo)
                            act.wait_ge(s_turn, b * TURNS + (used + 1))
                            a.copy(probT[:, j % 2, lo:lo + m, :].rearrange("p t c -> p (t c)"),
                                   turn[used % 2][:, 0:m * P]).then_inc(s_probT, 1)
                            used += 1
                act.wait_ge(s_big, b * RING + (R_XN2 + 1))
                a.copy(xT_hi[:, bass.ds(b * T, T)], big[R_XN2 % 2][:]).then_inc(s_hi2, 1)
            split_weights(0, 32)
            split_weights(1, 64)

            def position(s, par, bias, gates, after=True):
                for f in range(NF):
                    act.wait_ge(s_h, s * NF + (f + 1))
                    if after:
                        act.wait_ge(s_hilo, s * 2 + (f // 2 - 3))
                    a.activation(h[par][:, f, :], hbank[f], ACT.Gelu_apprx_tanh,
                                 bias=bias[:, f:f + 1]).then_inc(s_gelu, 1)
                if gates:
                    act.wait_ge(s_gbank, s + (1 - NC))
                    act.wait_ge(s_gated, s - 1)
                    a.copy(gate_bc[:, par, :], summ[0][:]).then_inc(s_gbc, 1)

            position(0, 0, cols[:, 0:NF], False, after=False)
            position(1, 1, cols[:, 0:NF], False, after=False)
            with nc.scalar.Fori(1, NC // 2) as cp:
                for j in range(2):
                    position(cp * 2 + j, j, cols[:, 0:NF], False)

            def expert(e, par, split):
                bias = bias_now[:, par, :]
                a.copy(bias, cols[:, bass.ds(e * NF, NF)]).then_inc(s_bias, 1)
                act.wait_ge(s_bias, e)
                position(e * NC, 0, bias, True)
                position(e * NC + 1, 1, bias, True)
                if split:
                    act.wait_ge(s_y, e * NC)
                    split_weights(1 - par, e * 32 + 64)
                with nc.scalar.Fori(1, NC // 2) as cp:
                    for j in range(2):
                        position(e * NC + (cp * 2 + j), j, bias, True)

            with nc.scalar.Fori(0, E // 2 - 1) as ep:
                expert(ep * 2 + 1, 1, True)
                expert(ep * 2 + 2, 0, True)
            expert(E - 1, 1, True)
            expert(E, 0, False)

        @block.tensor
        def _(pe):
            t = nc.tensor
            pe.wait_ge(s_const, 9)
            pe.wait_ge(s_w, 15 * 16)
            t.transpose(turn[0][:, 0:P], wvo[:, 0, :], ident[:]).then_inc(s_pe0, 1)
            t.transpose(turn[1][:, 0:NROWS], rows[:], ident[0:NROWS, 0:NROWS]).then_inc(s_pe0, 1)
            pe.wait_ge(s_act0, 2)
            t.matmul(turn[0][:, 0:P], wvo[:, 1, :], wvo[:, 2, :], start=True, stop=True).then_inc(s_pe0, 1)
            pe.wait_ge(s_act0, 5)

            with nc.tensor.Fori(0, B) as b:
                for i in range(TB):
                    pe.wait_ge(s_xn, b * (2 * TB) + (i + 1))
                    m = t.transpose(big[R_XN % 2][:, i * P:(i + 1) * P], xn[:, i, :], ident[:])
                m.then_inc(s_big, 1)
                pe.wait_ge(s_xnT, b + 1)
                for use, w in ((R_Q, 0), (R_QS, 1), (R_K, 2), (R_KS, 3)):
                    if use >= R_Q + 2:
                        pe.wait_ge(s_rot, b * 4 + (use - R_Q - 1))
                    for c in range(T // 512):
                        m = t.matmul(big[use % 2][:, c * 512:(c + 1) * 512], w4[:, w, :],
                                     xnT[:, c * 512:(c + 1) * 512], start=True, stop=True)
                    m.then_inc(s_big, 1)
                pe.wait_ge(s_rot, b * 4 + 3)
                for i in range(TB):
                    m = t.matmul(big[R_V % 2][:, i * P:(i + 1) * P], xnT[:, i * P:(i + 1) * P], wp[:],
                                 start=True, stop=True)
                m.then_inc(s_big, 1)

                def scores(i):
                    if i == 0:
                        pe.wait_ge(s_qk, b * 2 + 2)
                    elif i == 1:
                        pe.wait_ge(s_v, b + 1)
                    else:
                        pe.wait_ge(s_prob, b * TB + (i - 1))
                    slot = big[(R_S + i) % 2]
                    n = (i + 1) * P
                    for c in range(0, n, 512):
                        m = min(512, n - c)
                        t.matmul(slot[:, c:c + m], q[:, i * P:(i + 1) * P], k[:, c:c + m],
                                 start=True, stop=(c + m < n))
                    t.matmul(slot[:, i * P:n], ident_b[:], mask_b[:], start=False, stop=True).then_inc(s_big, 1)

                used = 0
                scores(0)
                for i in range(TB):
                    if i + 1 < TB:
                        scores(i + 1)
                    pe.wait_ge(s_prob, b * TB + (i + 1))
                    first = used
                    for lo in range(0, i + 1, 4):
                        if used >= 2:
                            pe.wait_ge(s_probT, b * TURNS + (used - 1))
                        for j in range(lo, min(lo + 4, i + 1)):
                            m = t.transpose(turn[used % 2][:, (j - lo) * P:(j - lo + 1) * P],
                                            prob[:, i % 2, j * P:(j + 1) * P], ident[:])
                        m.then_inc(s_turn, 1)
                        used += 1
                    if i >= 2:
                        pe.wait_ge(s_x2, b * TB + (i - 1))
                    for j in range(i + 1):
                        if j % 4 == 0:
                            pe.wait_ge(s_probT, b * TURNS + (first + j // 4 + 1))
                        m = t.matmul(summ[i % 2][:, 0:P], probT[:, i % 2, j, :], v[:, j, :],
                                     start=(j == 0), stop=(j == i))
                    m.then_inc(s_att, 1)
                for i in range(TB):
                    pe.wait_ge(s_xn, b * (2 * TB) + (TB + i + 1))
                    m = t.transpose(big[R_XN2 % 2][:, i * P:(i + 1) * P], xn[:, i, :], ident[:])
                m.then_inc(s_big, 1)
                pe.wait_ge(s_hi2, b + 1)
                pe.wait_ge(s_lo2, b + 1)
                for c in range(T // 512):
                    at = bass.ds(b * T + c * 512, 512)
                    for n, (gg, xx) in enumerate(((gw_hi, xT_hi), (gw_hi, xT_lo), (gw_lo, xT_hi))):
                        m = t.matmul(big[R_LG % 2][:, c * 512:(c + 1) * 512], gg[:], xx[:, at],
                                     start=(n == 0), stop=(n == 2))
                m.then_inc(s_big, 1)
                pe.wait_ge(s_lg, b + 1)
                for i in range(TB):
                    m = t.matmul(summ[0][:, i * E:(i + 1) * E], lgT[:, i * P:(i + 1) * P], ident[:, 0:E],
                                 start=True, stop=True)
                m.then_inc(s_lgT, 1)

            def split_products(out_ap, w, at, xs, first, last):
                for n, (ww, xx) in enumerate(((w_hi, xs[0]), (w_hi, xs[1]), (w_lo, xs[0]))):
                    m = t.matmul(out_ap, ww[:, w, at:at + P], xx, start=(first and n == 0), stop=(last and n == 2))
                return m

            def hidden(c, s, w, f, first=False):
                if not first:
                    pe.wait_ge(s_gelu, s * NF + (f + 1 - NF))
                at = bass.ds(c * CH, CH)
                split_products(hbank[f], w, f * P, (xT_hi[:, at], xT_lo[:, at]), True, True).then_inc(s_h, 1)

            def output(s, w, par, f):
                if f % 2 == 0:
                    pe.wait_ge(s_hilo, s * 2 + (f // 2 + 1))
                m = split_products(turn[par][:], w, F + f * P, (h_hi[:, par, f, :], h_lo[:, par, f, :]),
                                   f == 0, f == NF - 1)
                if f == NF - 1:
                    m.then_inc(s_y, 1)

            pe.wait_ge(s_wlo, 1)
            for f in range(NF):
                hidden(0, 0, 0, f, first=True)

            def count(n):
                pe.wait_ge(s_cnt, n)
                t.matmul(summ[1][:, 0:1], ones_b[:], count_b[:], start=True, stop=True).then_inc(s_tot, 1)

            with nc.tensor.Fori(0, NBIT // 10) as r:
                for j in range(2):
                    s, par = r * 2 + (1 + j), (1 + j) % 2
                    n = r * 10 + 5 * j
                    hidden(s, s, 0, 0)
                    count(n + 1)
                    for f in range(1, NF):
                        hidden(s, s, 0, f)
                    count(n + 2)
                    output(s - 1, 0, 1 - par, 0)
                    output(s - 1, 0, 1 - par, 1)
                    count(n + 3)
                    output(s - 1, 0, 1 - par, 2)
                    count(n + 4)
                    output(s - 1, 0, 1 - par, 3)
                    count(n + 5)
            for f in range(NF):
                hidden(NC - 1, NC - 1, 0, f)
            for f in range(NF):
                output(NC - 2, 0, 0, f)
            count(NBIT + 1)
            pe.wait_ge(s_cnt, NBIT + 2)
            t.matmul(summ[0][:, 0:E * NT], before_b[:], eq_b[:], start=True, stop=True)
            t.matmul(summ[0][:, E * NT:2 * E * NT], ones_b[:], eq_b[:], start=True, stop=True).then_inc(s_tot, 1)
            pe.wait_ge(s_gp, 1)
            for n in range(4):
                if n >= 2:
                    pe.wait_ge(s_gTc, n - 1)
                for i in range(NT // 4):
                    m = t.transpose(summ[n % 2][0:3 * E, :].bitcast(BF16)[:, i * P:(i + 1) * P],
                                    g_parts[:, n * (NT // 4) + i, :, :].rearrange("p a e -> p (a e)"), ident_b[:])
                m.then_inc(s_gt, 1)

            def position(e, c, s, w, par, w_before):
                for f in range(NF):
                    hidden(c, s, w, f)
                pe.wait_ge(s_gbc, s + (1 - NC))
                t.matmul(summ[0][:], pick_b[:, bass.ds(e - 1, 1), :].rearrange("p a m -> p (a m)"),
                         gT[:, bass.ds(c * CH, CH)], start=True, stop=True).then_inc(s_gbank, 1)
                for f in range(NF):
                    output(s - 1, w_before, 1 - par, f)

            def expert(e, w):
                pe.wait_ge(s_wlo, e + 1)
                position(e, 0, e * NC, w, 0, 1 - w)
                position(e, 1, e * NC + 1, w, 1, w)
                with nc.tensor.Fori(1, NC // 2) as cp:
                    for j in range(2):
                        position(e, cp * 2 + j, e * NC + (cp * 2 + j), w, j, w)

            with nc.tensor.Fori(0, E // 2) as ep:
                expert(ep * 2 + 1, 1)
                expert(ep * 2 + 2, 0)
            for f in range(NF):
                output(NE * NC - 1, 0, 1, f)
            for b in range(B):
                if b == 0:
                    pe.wait_ge(s_gelu, NE * NC * NF)
                pe.wait_ge(s_acc, 2 + NC * E + 2 * (b + 1))
                if b >= 2:
                    pe.wait_ge(s_res, b - 1)
                for i in range(TB):
                    m = t.transpose(big[b % 2][:, i * P:(i + 1) * P],
                                    outT[:, (b * TB + i) * P:(b * TB + i + 1) * P], ident[:])
                m.then_inc(s_fin, 1)

        @block.vector
        def _(dve):
            vec = nc.vector

            class Chain:

                def __init__(self, base):
                    self.base, self.n = base, 0

                def then(self, ins):
                    self.n += 1
                    ins.then_inc(s_dve, 1)
                    dve.wait_ge(s_dve, self.base + self.n)

            start = Chain(0)
            for n in range(NBIT):
                m = vec.memset(bit[:, n:n + 1], 1 << (NBIT - 1 - n))
            start.then(m)
            start.then(vec.memset(found[:], 0))
            dve.wait_ge(s_act0, 4)
            vec.tensor_tensor(gw_lo[:, 0:E], cols[:, ROWS_GW:NROWS], gw_hi[:, 0:E].bitcast(F32),
                              ALU.subtract).then_inc(s_gw, 1)

            def tile_of(b, i):
                return x2[:, bass.ds(b * TB + i, 1), :].rearrange("p a d -> p (a d)")

            def normalise(b, chain):
                vec.memset(nw[:, 3, 0:1], 0.0)
                for i in range(TB):
                    m = vec.bn_aggr(mv[:, i, :], stats[:, i, :])
                chain.then(m)
                w, y, z = nw[:, 0, :], nw[:, 1, :], nw[:, 2, :]
                chain.then(vec.tensor_scalar(w, mv[:, :, 1], EPS, None, ALU.add))
                chain.then(vec.tensor_scalar(nwi[:], w.bitcast(I32), 1, None, ALU.logical_shift_right))
                chain.then(vec.tensor_scalar(y.bitcast(I32), nwi[:], -1.0, float(RSQRT_MAGIC), ALU.mult, ALU.add))
                for _ in range(3):
                    chain.then(vec.tensor_tensor(z, y, w, ALU.mult))
                    chain.then(vec.scalar_tensor_tensor(z, z, -0.5, y, ALU.mult, ALU.mult))
                    chain.then(vec.scalar_tensor_tensor(y, z, 1.5, y, ALU.add, ALU.mult))
                for i in range(TB):
                    vec.tensor_scalar(xn[:, i, :], tile_of(b, i), mv[:, i, 0:1], nw[:, 1, i:i + 1],
                                      ALU.subtract, ALU.mult).then_inc(s_xn, 1)

            LINKS = 2 * (1 + 1 + 3 + 9) + TB
            first = start.n
            with nc.vector.Fori(0, B) as b:
                chain = Chain(b * LINKS + first)
                dve.wait_ge(s_x, b * 16 + 16)
                for i in range(TB):
                    m = vec.bn_stats(stats[:, i, :], tile_of(b, i))
                chain.then(m)
                normalise(b, chain)
                for use, dst, tab in ((R_Q, q, costab), (R_QS, qk_sin, sintab),
                                      (R_K, k, costab), (R_KS, qk_sin, sintab)):
                    dve.wait_ge(s_big, b * RING + (use + 1))
                    if use == R_KS:
                        dve.wait_ge(s_qk, b * 2 + 1)
                    vec.tensor_tensor(dst[:], big[use % 2][:], tab[:], ALU.mult).then_inc(s_rot, 1)

                def row_max(i):
                    dve.wait_ge(s_big, b * RING + (R_S + i + 1))
                    vec.tensor_reduce(neg_max[:, i:i + 1], big[(R_S + i) % 2][:, 0:(i + 1) * P], AX.X, ALU.max,
                                      negate=True).then_inc(s_max, 1)

                row_max(0)
                for i in range(TB):
                    if i + 1 < TB:
                        row_max(i + 1)
                    if i:
                        dve.wait_ge(s_x2, b * TB + i)
                    dve.wait_ge(s_prob, b * TB + (i + 1))
                    chain.then(vec.reciprocal(row_inv[:, i:i + 1], row_sum[:, i:i + 1]))
                    dve.wait_ge(s_att, b * TB + (i + 1))
                    vec.scalar_tensor_tensor(tile_of(b, i), summ[i % 2][:, 0:P], row_inv[:, i:i + 1],
                                             tile_of(b, i), ALU.mult, ALU.add).then_inc(s_x2, 1)
                    if i:
                        vec.bn_stats(stats[:, i - 1, :], tile_of(b, i - 1))
                dve.wait_ge(s_x2, b * TB + TB)
                vec.memset(nw[:, 3, 0:1], 0.0)
                chain.then(vec.bn_stats(stats[:, TB - 1, :], tile_of(b, TB - 1)))
                normalise(b, chain)
                assert chain.n == LINKS, chain.n
                dve.wait_ge(s_big, b * RING + (R_XN2 + 1))
                dve.wait_ge(s_hi2, b + 1)
                at = bass.ds(b * T, T)
                vec.tensor_tensor(xT_lo[:, at], big[R_XN2 % 2][:], xT_hi[:, at].bitcast(F32),
                                  ALU.subtract).then_inc(s_lo2, 1)
                dve.wait_ge(s_big, b * RING + (R_LG + 1))
                vec.tensor_copy(lgT[:], big[R_LG % 2][:]).then_inc(s_lg, 1)
                dve.wait_ge(s_lgT, b + 1)
                vec.tensor_copy(lg[:, :, bass.ds(b * TB, TB)],
                                summ[0][:, 0:TB * E].rearrange("p (t e) -> p e t", e=E)).then_inc(s_lgc, 1)

            base = first + B * LINKS

            def hi_part(s, par, half):
                dve.wait_ge(s_gelu, s * NF + (2 * half + 2))
                fs = slice(2 * half, 2 * half + 2)
                vec.tensor_copy(h_hi[:, par, fs, :], h[par][:, fs, :]).then_inc(s_hp, 1)

            def lo_part(s, par, half):
                dve.wait_ge(s_hp, s * 2 + (half + 1))
                fs = slice(2 * half, 2 * half + 2)
                vec.tensor_tensor(h_lo[:, par, fs, :], h[par][:, fs, :], h_hi[:, par, fs, :].bitcast(F32),
                                  ALU.subtract).then_inc(s_hilo, 1)

            def gate(s, e, par, slot):
                dve.wait_ge(s_y, s + 1)
                dve.wait_ge(s_acc, s + 1)
                vec.scalar_tensor_tensor(gated[:, par, :], turn[par][:], cols[:, bass.ds(ROWS_B2 + e, 1)],
                                         gate_bc[:, slot, :], ALU.add, ALU.mult).then_inc(s_gated, 1)

            chain = Chain(base)
            hi_part(0, 0, 0)
            hi_part(0, 0, 1)
            lo_part(0, 0, 0)
            lo_part(0, 0, 1)
            dve.wait_ge(s_lgc, B)
            by_token = "p e t -> p t e"

            def spread(v_):
                return v_.unsqueeze(1).to_broadcast([P, E, NT])

            chain.then(vec.tensor_reduce(rs[:, 0, :], lg[:].rearrange(by_token), AX.X, ALU.max))
            chain.then(vec.tensor_tensor(ra[:], lg[:], spread(rs[:, 0, :]), ALU.subtract))
            chain.then(vec.tensor_scalar(ra[:], ra[:], -100.0, None, ALU.max))
            chain.then(vec.tensor_scalar(rb[:], ra[:], LOG2E, ROUND, ALU.mult, ALU.add))
            chain.then(vec.tensor_scalar(rb[:], rb[:], ROUND, -127.0, ALU.subtract, ALU.max))
            chain.then(vec.tensor_scalar(pow2[:], rb[:], 127.0, 8388608.0, ALU.add, ALU.mult))
            chain.then(vec.scalar_tensor_tensor(ra[:], rb[:], -LN2_HI, ra[:], ALU.mult, ALU.add))
            chain.then(vec.scalar_tensor_tensor(ra[:], rb[:], -LN2_LO, ra[:], ALU.mult, ALU.add))
            fact = [1.0, 1.0, 2.0, 6.0, 24.0, 120.0, 720.0, 5040.0]
            chain.then(vec.tensor_scalar(rb[:], ra[:], 1.0 / fact[7], None, ALU.mult))
            for d in range(6, 0, -1):
                chain.then(vec.scalar_tensor_tensor(rb[:], rb[:], 1.0 / fact[d], ra[:], ALU.add, ALU.mult))
            chain.then(vec.scalar_tensor_tensor(rb[:], rb[:], 1.0, pow2[:].bitcast(F32), ALU.add, ALU.mult))
            chain.then(vec.tensor_reduce(rs[:, 0, :], rb[:].rearrange(by_token), AX.X, ALU.add))
            chain.then(vec.reciprocal(rs[:, 1, :], rs[:, 0, :]))
            chain.then(vec.tensor_tensor(lg[:], rb[:], spread(rs[:, 1, :]), ALU.mult))
            flat = "p e t -> p (e t)"
            scores, ra_ = lg[:].rearrange(flat), ra[:].rearrange(flat)

            def bit_try(n, chain):
                b_n = bit[:, bass.ds(n, 1)]
                chain.then(vec.tensor_tensor(cand[:], found[:], b_n, ALU.bitwise_or))
                vec.tensor_scalar(ra_, scores, cand[:].bitcast(F32), None, ALU.is_ge, ALU.add,
                                  accum_out=count_b[:]).then_inc(s_cnt, 1)

            def bit_keep(n, chain):
                dve.wait_ge(s_tot, n + 1)
                chain.then(vec.tensor_scalar(flag[:], summ[1][:, 0:1], float(K_TOP), bit[:, bass.ds(n, 1)],
                                             ALU.is_ge, ALU.mult))
                chain.then(vec.tensor_tensor(found[:], found[:], flag[:], ALU.bitwise_or))

            base += chain.n
            with nc.vector.Fori(0, NBIT // 10) as r:
                chain = Chain(r * 30 + base)
                for j in range(2):
                    s, par = r * 2 + (1 + j), (1 + j) % 2
                    for n, work in enumerate((hi_part, lo_part, hi_part, lo_part, None)):
                        bit_try(r * 10 + (5 * j + n), chain)
                        if work:
                            work(s, par, n // 2)
                        else:
                            gate(s - 1, 0, 1 - par, 1)
                        bit_keep(r * 10 + (5 * j + n), chain)
                assert chain.n == 30
            chain = Chain(base + 3 * NBIT)
            limit = found[:].bitcast(F32)
            vec.tensor_scalar(ra_, scores, limit, None, ALU.is_gt, ALU.add, accum_out=count_b[:]).then_inc(s_cnt, 1)
            vec.tensor_scalar(eq_b[:], scores, limit, None, ALU.is_equal).then_inc(s_cnt, 1)
            for half in range(2):
                hi_part(NC - 1, 1, half)
                lo_part(NC - 1, 1, half)
            gate(NC - 2, 0, 0, 1)
            dve.wait_ge(s_tot, NBIT + 2)
            before, inside = summ[0][:, 0:E * NT], summ[0][:, E * NT:2 * E * NT]
            chain.then(vec.tensor_tensor_scan(ra_, inside, zeros[:], 0.0, ALU.add, ALU.add))
            chain.then(vec.tensor_tensor(ra_, ra_, inside, ALU.subtract))
            chain.then(vec.tensor_tensor(ra_, ra_, before, ALU.add))
            chain.then(vec.tensor_copy(count_f[:, 0:1], summ[1][:, 0:1]))
            chain.then(vec.tensor_scalar(ra_, ra_, count_f[:, 0:1], float(K_TOP), ALU.add, ALU.is_lt))
            chain.then(vec.tensor_tensor(ra_, ra_, eq_b[:], ALU.mult))
            chain.then(vec.scalar_tensor_tensor(ra_, scores, limit, ra_, ALU.is_gt, ALU.add))
            chain.then(vec.tensor_tensor(ra_, ra_, scores, ALU.mult))
            part = [g_parts[:, :, n, :].rearrange("p t e -> p e t") for n in range(3)]
            chain.then(vec.tensor_copy(part[0], ra[:]))
            chain.then(vec.tensor_tensor(rb[:], ra[:], part[0], ALU.subtract))
            chain.then(vec.tensor_copy(part[1], rb[:]))
            chain.then(vec.tensor_tensor(ra[:], rb[:], part[1], ALU.subtract))
            vec.tensor_copy(part[2], ra[:]).then_inc(s_gp, 1)
            for n in range(4):
                dve.wait_ge(s_gt, n + 1)
                m = vec.tensor_copy(gT[0:3 * E, n * (S // 4):(n + 1) * (S // 4)],
                                    summ[n % 2][0:3 * E, :].bitcast(BF16))
                m.then_inc(s_gTc, 1)
            dve.wait_ge(s_gTc, 4)
            vec.tensor_copy(count_f[:, 1:2], count_f[:, 0:1]).then_inc(s_gbc, 1)

            def position(e, s, par, first):
                for half in range(2):
                    hi_part(s, par, half)
                    lo_part(s, par, half)
                if not first:
                    dve.wait_ge(s_gbc, s + (1 - NC))
                    gate(s - 1, e, 1 - par, 1 - par)
                else:
                    dve.wait_ge(s_gbc, s + (1 - NC))
                    gate(s - 1, e - 1, 1 - par, 1 - par)

            def expert(e):
                position(e, e * NC, 0, True)
                position(e, e * NC + 1, 1, False)
                with nc.vector.Fori(1, NC // 2) as cp:
                    for j in range(2):
                        position(e, e * NC + (cp * 2 + j), j, False)

            with nc.vector.Fori(0, E // 2) as ep:
                expert(ep * 2 + 1)
                expert(ep * 2 + 2)
            dve.wait_ge(s_gbc, NE * NC + (1 - NC))
            gate(NE * NC - 1, E, 1, 1)
            for b in range(B):
                dve.wait_ge(s_fin, b + 1)
                o = x2[:, b * TB:(b + 1) * TB, :].rearrange("p t d -> p (t d)")
                vec.tensor_tensor(o, o, big[b % 2][:], ALU.add).then_inc(s_res, 1)


def rotation_tables(T, D, base=10000.0):
    import numpy as np
    half = D // 2
    freqs = np.power(np.float32(base), -np.arange(half, dtype=np.float32) / np.float32(half)).astype(np.float32)
    angles = (freqs[:, None] * np.arange(T, dtype=np.float32)[None, :]).astype(np.float32)
    cos, sin = np.cos(angles).astype(np.float32), np.sin(angles).astype(np.float32)
    return np.concatenate([cos, cos]), np.concatenate([-sin, sin])


_INS = ['L0_attn_x', 'L0_attn_wq', 'L0_attn_wk', 'L0_attn_wv', 'L0_attn_wo', 'L0_ffn_gate_weight', 'L0_ffn_W1',
        'L0_ffn_b1', 'L0_ffn_W2', 'L0_ffn_b2', 'L0_ffn_Ws1', 'L0_ffn_bs1', 'L0_ffn_Ws2', 'L0_ffn_bs2']


def kernel(**inputs):
    import numpy as np
    import concourse.bacc as bacc
    from concourse.bass_utils import run_bass_kernel_spmd

    nc = bacc.Bacc("TRN2", target_bir_lowering=False, num_devices=1)
    arrays = {name: np.ascontiguousarray(inputs[name]) for name in _INS}
    B, T, D = arrays['L0_attn_x'].shape
    arrays['cos'], arrays['sin'] = rotation_tables(T, D)
    args = [nc.dram_tensor(name, a.shape, mybir.dt.from_np(a.dtype), kind="ExternalInput").ap()
            for name, a in arrays.items()]
    args.append(nc.dram_tensor("out", (B, T, D), F32, kind="ExternalOutput").ap())
    moe_layer(nc, *args)
    r = run_bass_kernel_spmd(nc, [arrays], core_ids=[0])
    return r.results[0]["out"]
```

```python
from contextlib import ExitStack

import concourse.bass as bass
from concourse import mybir

ALU = mybir.AluOpType
ACT = mybir.ActivationFunctionType
AX = mybir.AxisListType
F32 = mybir.dt.float32
F32R = mybir.dt.float32r
BF16 = mybir.dt.bfloat16
I32 = mybir.dt.int32

P = 128
EPS = 1e-5
MASKED = -1e30
LOG2E = 1.4426950408889634
LN2_HI = 0.693359375
LN2_LO = -2.12194440e-4
ROUND = 12582912.0
RSQRT_MAGIC = 0x5F3759DF


def moe_layer(nc, x_in, wq_in, wk_in, wv_in, wo_in, gate_in, W1_in, b1_in, W2_in, b2_in,
              Ws1_in, bs1_in, Ws2_in, bs2_in, cos_in, sin_in, out):
    B, T, D = x_in.shape
    E, _, F = W1_in.shape
    assert D == P and F % P == 0 and T % 512 == 0
    TB = T // P
    NT = B * TB
    S = B * T
    NF = F // P
    K_TOP = 2 * S
    CH = 512
    NC = S // CH
    NE = E + 1
    QK_SCALE = 1.0 / D
    NBIT = 30
    assert NC == 8 and E % 2 == 0 and TB == 8 and NBIT == 5 * (NC - 2)

    ORDER = [TB - 1 - n // 2 if n % 2 == 0 else n // 2 for n in range(TB)]
    TURNS = sum((i + 4) // 4 for i in range(TB))

    ROWS_B1, ROWS_B2, ROWS_GW = 0, NE * NF, NE * NF + NE
    NROWS = ROWS_GW + E

    with ExitStack() as ctx:
        def sb(name, shape, dt):
            return ctx.enter_context(nc.sbuf_tensor(name, shape, dt))

        def pb(name, shape, dt):
            return ctx.enter_context(nc.psum_tensor(name, shape, dt))

        def sem(name):
            return ctx.enter_context(nc.semaphore(name))

        ident = sb("ident", [P, P], F32)
        ident_b = sb("ident_b", [P, P], BF16)
        mask_b = sb("mask_b", [P, P], BF16)
        before_b = sb("before_b", [P, P], BF16)
        ones_b = sb("ones_b", [P, P], BF16)
        pick_b = sb("pick_b", [P, E, P], BF16)
        costab = sb("costab", [P, T], F32)
        sintab = sb("sintab", [P, T], F32)
        w4 = sb("w4", [P, 4, D], F32)
        wvo = sb("wvo", [P, 3, D], F32)
        wp = sb("wp", [P, D], F32)
        rows = sb("rows", [NROWS, P], F32)
        cols = sb("cols", [P, NROWS], F32)
        gw_hi = sb("gw_hi", [P, P], F32R)
        gw_lo = sb("gw_lo", [P, P], F32R)
        x2 = sb("x2", [P, NT, D], F32)
        xn = sb("xn", [P, TB, D], F32)
        xn2 = sb("xn2", [P, TB, D], F32)
        xnT = sb("xnT", [P, T], F32)
        q = sb("q", [P, T], F32)
        k = sb("k", [P, T], F32)
        v = sb("v", [P, TB, D], F32)
        prob = sb("prob", [P, 2, T], F32)
        probT = sb("probT", [P, 2, TB, P], F32)
        neg_max = sb("neg_max", [P, TB], F32)
        row_sum = sb("row_sum", [P, TB], F32)
        row_inv = sb("row_inv", [P, TB], F32)
        stats = sb("stats", [P, NT, 6], F32)
        mv = sb("mv", [P, NT, 2], F32)
        stats2 = sb("stats2", [P, TB, 6], F32)
        mv2 = sb("mv2", [P, TB, 2], F32)
        inv1 = sb("inv1", [P, NT], F32)
        inv2 = sb("inv2", [P, TB], F32)
        nw = sb("nw", [P, 3, NT], F32)
        nwi = sb("nwi", [P, NT], I32)
        xT_hi = sb("xT_hi", [P, S], F32R)
        xT_lo = sb("xT_lo", [P, S], F32R)
        lg = sb("lg", [P, E, NT], F32)
        ra = sb("ra", [P, E, NT], F32)
        rb = sb("rb", [P, E, NT], F32)
        pow2 = sb("pow2", [P, E, NT], I32)
        rs = sb("rs", [P, 2, NT], F32)
        bit = sb("bit", [P, 32], I32)
        found = sb("found", [P, 1], I32)
        cand = sb("cand", [P, 1], I32)
        flag = sb("flag", [P, 1], I32)
        count_b = sb("count_b", [P, 1], BF16)
        count_f = sb("count_f", [P, 2], F32)
        eq_b = sb("eq_b", [P, E * NT], BF16)
        zeros = sb("zeros", [P, E * NT], F32)
        g_parts = sb("g_parts", [P, NT, 3, E], BF16)
        gT = sb("gT", [P, S], BF16)
        lgT = sb("lgT", [P, T], F32)
        w_raw = sb("w_raw", [P, 2, 2 * F], F32)
        w_hi = sb("w_hi", [P, 2, 2 * F], F32R)
        w_lo = sb("w_lo", [P, 2, 2 * F], F32R)
        h = [prob[:].rearrange("p a (f c) -> p (a f) c", c=CH), probT[:].rearrange("p a (f t) c -> p (a f) (t c)", f=2)]
        h_hi = sb("h_hi", [P, 2, NF, CH], F32R)
        h_lo = sb("h_lo", [P, 2, NF, CH], F32R)
        bias_now = sb("bias_now", [P, 2, NF], F32)
        gate_bc = sb("gate_bc", [P, 2, CH], F32)
        nothing_v = sb("nothing_v", [P, 1], F32)
        gated = sb("gated", [P, 2, CH], F32)
        outT = sb("outT", [P, S], F32)

        q_cos, q_sin, k_cos, k_sin = (outT[:, n * T:(n + 1) * T] for n in range(4))

        big = [pb(f"big{i}", [P, 1024], F32) for i in range(2)]
        turn = [pb(f"turn{i}", [P, 512], F32) for i in range(2)]
        summ = [pb(f"summ{i}", [P, 512], F32) for i in range(2)]
        hbank = [big[f // 2][:, (f % 2) * 512:(f % 2) * 512 + 512] for f in range(NF)]

        s_w = sem("attention_weights_loaded")
        s_x = sem("x_loaded")
        s_const = sem("constants_ready")
        s_pe0 = sem("setup_products_done")
        s_act0 = sem("setup_copies_done")
        s_xr = sem("x_of_later_batches_loaded")
        s_xn = sem("normed1_ready")
        s_xn2 = sem("normed2_ready")
        s_xnp = sem("normed1_turned")
        s_xnT = sem("normed1_turned_copied")
        s_xn2p = sem("normed2_turned")
        s_proj = sem("projection_summed")
        s_vp = sem("values_summed")
        s_lgp = sem("logits_summed")
        s_s = sem("scores_summed")
        s_rot = sem("rotation_part_ready")
        s_qk = sem("query_or_key_ready")
        s_v = sem("values_ready")
        s_max = sem("row_max_ready")
        s_prob = sem("probs_ready")
        s_turn = sem("probs_turned")
        s_probT = sem("turned_probs_copied")
        s_att = sem("attention_tile_summed")
        s_x2 = sem("attention_added")
        s_hi2 = sem("normed2_hi_ready")
        s_lo2 = sem("normed2_lo_ready")
        s_lg = sem("logits_copied")
        s_lgT = sem("logits_turned")
        s_lgc = sem("logits_by_token_ready")
        s_gw = sem("gate_weight_ready")
        s_raw = sem("expert_weights_loaded")
        s_whi = sem("expert_weights_hi_ready")
        s_wlo = sem("expert_weights_lo_ready")
        s_bias = sem("expert_bias_copied")
        s_h = sem("hidden_chunk_summed")
        s_gelu = sem("gelu_chunk_ready")
        s_hp = sem("hidden_hi_ready")
        s_hilo = sem("hidden_split_ready")
        s_y = sem("expert_step_summed")
        s_gbank = sem("gate_rows_spread")
        s_gbc = sem("gate_rows_copied")
        s_gated = sem("expert_step_gated")
        s_acc = sem("expert_step_added")
        s_cnt = sem("count_ready")
        s_tot = sem("count_summed")
        s_gp = sem("gate_parts_ready")
        s_gt = sem("gate_parts_turned")
        s_gTc = sem("gate_parts_copied")
        s_fin = sem("result_turned")
        s_res = sem("result_added")
        s_out = sem("result_stored")
        s_dve = sem("vector_chain")
        s_pool0 = sem("pool_chain")

        block = ctx.enter_context(nc.Block())

        @block.sync
        def _(sp):
            sp.dma_start(x2[:, 0:TB, :], x_in[0, :, :].rearrange("(t p) d -> p t d", p=P)).then_inc(s_x, 16)
            sp.dma_start(x2[:, TB:NT, :],
                         x_in[1:B, :, :].rearrange("b (t p) d -> p (b t) d", p=P)).then_inc(s_xr, 16)

            def load_expert(par, w1, w2):
                sp.dma_start(w_raw[:, par, 0:F], w1).then_inc(s_raw, 16)
                sp.dma_start(w_raw[:, par, F:2 * F].rearrange("p (c d) -> p c d", d=D), w2).then_inc(s_raw, 16)

            def w1_of(e):
                return W1_in[bass.ds(e, 1), :, :].rearrange("a d f -> d (a f)")

            def w2_of(e):
                return W2_in[bass.ds(e, 1), :, :].rearrange("a (c p) d -> p (a c) d", p=P)

            load_expert(0, Ws1_in, Ws2_in.rearrange("(c p) d -> p c d", p=P))
            sp.wait_ge(s_raw, 32)
            load_expert(1, w1_of(0), w2_of(0))
            with nc.sync.Fori(0, E // 2 - 1) as ep:
                for par in range(2):
                    sp.wait_ge(s_wlo, ep * 2 + (par + 2))
                    load_expert(par, w1_of(ep * 2 + (par + 1)), w2_of(ep * 2 + (par + 1)))
            sp.wait_ge(s_wlo, E)
            load_expert(0, w1_of(E - 1), w2_of(E - 1))
            for b in range(B):
                sp.wait_ge(s_res, b + 1)
                sp.dma_start(out[b, :, :].rearrange("(t p) d -> p t d", p=P),
                             x2[:, b * TB:(b + 1) * TB, :]).then_inc(s_out, 16)
            sp.wait_ge(s_out, 16 * B)

        @block.gpsimd
        def _(pool):
            g = nc.gpsimd
            n = [0]

            def then(ins):
                n[0] += 1
                ins.then_inc(s_pool0, 1)
                pool.wait_ge(s_pool0, n[0])

            then(g.memset(ident[:], 0.0))
            then(g.affine_select(out=ident[:], in_=ident[:], compare_op=ALU.not_equal, fill=1.0, base=0,
                                 pattern=[[-1, P]], channel_multiplier=1))
            g.tensor_copy(ident_b[:], ident[:]).then_inc(s_const, 1)
            then(g.memset(mask_b[:], 0.0))
            g.affine_select(out=mask_b[:], in_=mask_b[:], compare_op=ALU.is_ge, fill=MASKED, base=0,
                            pattern=[[-1, P]], channel_multiplier=1).then_inc(s_const, 1)
            g.memset(ones_b[:], 1.0).then_inc(s_const, 1)
            then(g.memset(before_b[:], 0.0))
            g.affine_select(out=before_b[:], in_=before_b[:], compare_op=ALU.is_ge, fill=1.0, base=0,
                            pattern=[[-1, P]], channel_multiplier=1).then_inc(s_const, 1)
            then(g.memset(pick_b[:], 0.0))
            for part in range(3):
                then(g.affine_select(out=pick_b[:], in_=pick_b[:], compare_op=ALU.not_equal, fill=1.0,
                                     base=-part * E, pattern=[[-1, E], [0, P]], channel_multiplier=1))
            g.memset(gw_hi[:].bitcast(F32), 0.0).then_inc(s_const, 1)
            g.memset(gw_lo[:].bitcast(F32), 0.0).then_inc(s_const, 1)
            g.memset(gT[:].bitcast(F32), 0.0).then_inc(s_const, 1)
            g.memset(gate_bc[:, 1, :], 1.0).then_inc(s_const, 1)
            g.memset(zeros[:], 0.0).then_inc(s_const, 1)

            def add_query(b):
                pool.wait_ge(s_rot, b * 4 + 2)
                g.tensor_tensor(q[:], q_cos, q_sin, ALU.add).then_inc(s_qk, 1)

            add_query(0)
            with nc.gpsimd.Fori(0, B - 1) as b:
                pool.wait_ge(s_s, b * TB + TB)
                add_query(b + 1)
            pool.wait_ge(s_qk, 2 * B)
            for half in range(2):
                g.memset(outT[:, half * (S // 2):(half + 1) * (S // 2)], 0.0).then_inc(s_acc, 1)

            def split_weights(par, n_whi):
                pool.wait_ge(s_whi, n_whi)
                g.tensor_tensor(w_lo[:, par, :], w_raw[:, par, :], w_hi[:, par, :].bitcast(F32),
                                ALU.subtract).then_inc(s_wlo, 1)

            def accumulate(done, c, par):
                pool.wait_ge(s_gated, done + 1)
                o = outT[:, bass.ds(c * CH, CH)]
                g.tensor_tensor(o, o, gated[:, par, :], ALU.add).then_inc(s_acc, 1)

            split_weights(0, 1)
            split_weights(1, 2)
            pool.wait_ge(s_acc, 2)
            with nc.gpsimd.Fori(0, NC // 2) as cp:
                for j in range(2):
                    accumulate(cp * 2 + j, cp * 2 + j, j)

            def expert(e, par, split):
                for j in range(2):
                    accumulate(e * NC + j, j, j)
                if split:
                    split_weights(1 - par, e + 2)
                with nc.gpsimd.Fori(1, NC // 2) as cp:
                    for j in range(2):
                        accumulate(e * NC + (cp * 2 + j), cp * 2 + j, j)

            with nc.gpsimd.Fori(0, E // 2 - 1) as ep:
                expert(ep * 2 + 1, 1, True)
                expert(ep * 2 + 2, 0, True)
            expert(E - 1, 1, True)
            expert(E, 0, False)

        @block.scalar
        def _(act):
            a = nc.scalar
            H = D // 2
            for j, w in ((0, wq_in), (2, wk_in)):
                w = w.rearrange("h m d -> m (h d)")
                act.dma_start(w4[:, j, :], w).then_inc(s_w, 16)
                act.dma_start(w4[:, j + 1, 0:H], w[:, H:D]).then_inc(s_w, 16)
                act.dma_start(w4[:, j + 1, H:D], w[:, 0:H]).then_inc(s_w, 16)
            act.dma_start(wvo[:, 0, :], wv_in.rearrange("h m d -> m (h d)")).then_inc(s_w, 16)
            act.dma_start(wvo[:, 2, :], wo_in.rearrange("h d m -> d (h m)")).then_inc(s_w, 16)
            act.dma_start(rows[ROWS_B1:ROWS_B1 + NF, :], bs1_in.rearrange("(c p) -> c p", p=P)).then_inc(s_w, 16)
            act.dma_start(rows[ROWS_B1 + NF:ROWS_B2, :], b1_in.rearrange("e (c p) -> (e c) p", p=P)).then_inc(s_w, 16)
            act.dma_start(rows[ROWS_B2:ROWS_B2 + 1, :], bs2_in.rearrange("(a p) -> a p", a=1)).then_inc(s_w, 16)
            act.dma_start(rows[ROWS_B2 + 1:ROWS_GW, :], b2_in).then_inc(s_w, 16)
            act.dma_start(rows[ROWS_GW:NROWS, :], gate_in).then_inc(s_w, 16)
            act.dma_start(costab[:], cos_in).then_inc(s_w, 16)
            act.dma_start(sintab[:], sin_in).then_inc(s_w, 16)
            act.wait_ge(s_w, 15 * 16)
            a.mul(w4[:, 0:2, :], w4[:, 0:2, :], QK_SCALE).then_inc(s_act0, 1)
            act.wait_ge(s_pe0, 1)
            a.copy(wvo[:, 1, :], turn[0][:, 0:P]).then_inc(s_act0, 1)
            act.wait_ge(s_pe0, 2)
            a.copy(cols[:], turn[1][:, 0:NROWS]).then_inc(s_act0, 1)
            act.wait_ge(s_act0, 3)
            act.wait_ge(s_const, 6)
            a.copy(gw_hi[:, 0:E], cols[:, ROWS_GW:NROWS]).then_inc(s_act0, 1)
            act.wait_ge(s_pe0, 3)
            a.copy(wp[:], turn[0][:, 0:P]).then_inc(s_act0, 1)

            def split_weights(par, n_raw):
                act.wait_ge(s_raw, n_raw)
                a.copy(w_hi[:, par, :], w_raw[:, par, :]).then_inc(s_whi, 1)

            def turn_copy(b):
                act.wait_ge(s_xnp, b + 1)
                a.copy(xnT[:], big[1][:]).then_inc(s_xnT, 1)

            def hi_copy(b):
                act.wait_ge(s_xn2p, b + 1)
                a.copy(xT_hi[:, bass.ds(b * T, T)], big[1][:]).then_inc(s_hi2, 1)

            def logits_copy(b):
                act.wait_ge(s_lgp, b + 1)
                a.copy(lgT[:], big[1][:]).then_inc(s_lg, 1)

            def exps(b, n):
                i = ORDER[n]
                act.wait_ge(s_max, b * TB + (n + 1))
                a.activation(prob[:, n % 2, 0:(i + 1) * P], big[0][:, 0:(i + 1) * P], ACT.Exp,
                             bias=neg_max[:, i:i + 1], accum_out=row_sum[:, i:i + 1]).then_inc(s_prob, 1)

            def batch(b, post, prep):
                exps(b, 0)
                act.wait_ge(s_vp, b + 1)
                a.copy(v[:].rearrange("p t d -> p (t d)"), big[1][:]).then_inc(s_v, 1)
                used = 0
                for n in range(TB):
                    i = ORDER[n]
                    if n >= 2:
                        act.wait_ge(s_att, b * TB + (n - 1))
                    for lo in range(0, i + 1, 4):
                        m = min(4, i + 1 - lo)
                        act.wait_ge(s_turn, b * TURNS + (used + 1))
                        a.copy(probT[:, n % 2, lo:lo + m, :].rearrange("p t c -> p (t c)"),
                               turn[used % 2][:, 0:m * P]).then_inc(s_probT, 1)
                        used += 1
                    if n + 1 < TB:
                        exps(b, n + 1)
                    if n == 0 and prep:
                        turn_copy(b + 1)
                    if n == 1 and post:
                        hi_copy(b - 1)
                    if n == 6 and post:
                        logits_copy(b - 1)

            turn_copy(0)
            batch(0, False, True)
            with nc.scalar.Fori(1, B - 1) as b:
                batch(b, True, True)
            batch(B - 1, True, False)
            hi_copy(B - 1)
            logits_copy(B - 1)
            split_weights(0, 32)
            split_weights(1, 64)

            def position(s, par, bias, gates, after=True):
                for f in range(NF):
                    act.wait_ge(s_h, s * NF + (f + 1))
                    if after:
                        act.wait_ge(s_hilo, s * 2 + (f // 2 - 3))
                    a.activation(h[par][:, f, :], hbank[f], ACT.Gelu_apprx_tanh,
                                 bias=bias[:, f:f + 1]).then_inc(s_gelu, 1)
                if gates:
                    act.wait_ge(s_gbank, s + (1 - NC))
                    act.wait_ge(s_gated, s - 1)
                    a.copy(gate_bc[:, par, :], summ[0][:]).then_inc(s_gbc, 1)

            position(0, 0, cols[:, 0:NF], False, after=False)
            position(1, 1, cols[:, 0:NF], False, after=False)
            with nc.scalar.Fori(1, NC // 2) as cp:
                for j in range(2):
                    position(cp * 2 + j, j, cols[:, 0:NF], False)

            def expert(e, par, split):
                bias = bias_now[:, par, :]
                a.copy(bias, cols[:, bass.ds(e * NF, NF)]).then_inc(s_bias, 1)
                act.wait_ge(s_bias, e)
                position(e * NC, 0, bias, True)
                position(e * NC + 1, 1, bias, True)
                if split:
                    act.wait_ge(s_y, e * NC)
                    split_weights(1 - par, e * 32 + 64)
                with nc.scalar.Fori(1, NC // 2) as cp:
                    for j in range(2):
                        position(e * NC + (cp * 2 + j), j, bias, True)

            with nc.scalar.Fori(0, E // 2 - 1) as ep:
                expert(ep * 2 + 1, 1, True)
                expert(ep * 2 + 2, 0, True)
            expert(E - 1, 1, True)
            expert(E, 0, False)

        @block.tensor
        def _(pe):
            t = nc.tensor
            pe.wait_ge(s_const, 9)
            pe.wait_ge(s_w, 15 * 16)
            t.transpose(turn[0][:, 0:P], wvo[:, 0, :], ident[:]).then_inc(s_pe0, 1)
            t.transpose(turn[1][:, 0:NROWS], rows[:], ident[0:NROWS, 0:NROWS]).then_inc(s_pe0, 1)
            pe.wait_ge(s_act0, 2)
            t.matmul(turn[0][:, 0:P], wvo[:, 1, :], wvo[:, 2, :], start=True, stop=True).then_inc(s_pe0, 1)
            pe.wait_ge(s_act0, 5)

            def turn_normed(b):
                for i in range(TB):
                    pe.wait_ge(s_xn, b * TB + (i + 1))
                    m = t.transpose(big[1][:, i * P:(i + 1) * P], xn[:, i, :], ident[:])
                m.then_inc(s_xnp, 1)

            def turn_normed2(b):
                for i in range(TB):
                    pe.wait_ge(s_xn2, b * TB + (i + 1))
                    m = t.transpose(big[1][:, i * P:(i + 1) * P], xn2[:, i, :], ident[:])
                m.then_inc(s_xn2p, 1)

            def project(w, slot):
                for c in range(T // 512):
                    m = t.matmul(big[slot][:, c * 512:(c + 1) * 512], w4[:, w, :],
                                 xnT[:, c * 512:(c + 1) * 512], start=True, stop=True)
                m.then_inc(s_proj, 1)

            def values():
                for i in range(TB):
                    m = t.matmul(big[1][:, i * P:(i + 1) * P], xnT[:, i * P:(i + 1) * P], wp[:],
                                 start=True, stop=True)
                m.then_inc(s_vp, 1)

            def logits(b):
                for c in range(T // 512):
                    at = bass.ds(b * T + c * 512, 512)
                    for n, (gg, xx) in enumerate(((gw_hi, xT_hi), (gw_hi, xT_lo), (gw_lo, xT_hi))):
                        m = t.matmul(big[1][:, c * 512:(c + 1) * 512], gg[:], xx[:, at],
                                     start=(n == 0), stop=(n == 2))
                m.then_inc(s_lgp, 1)

            def turn_logits(b):
                pe.wait_ge(s_lg, b + 1)
                for i in range(TB):
                    m = t.matmul(summ[0][:, 256 + i * E:256 + (i + 1) * E], lgT[:, i * P:(i + 1) * P],
                                 ident[:, 0:E], start=True, stop=True)
                m.then_inc(s_lgT, 1)

            def scores(b, n):
                i = ORDER[n]
                for c in range(0, (i + 1) * P, 512):
                    m = min(512, (i + 1) * P - c)
                    t.matmul(big[0][:, c:c + m], q[:, i * P:(i + 1) * P], k[:, c:c + m],
                             start=True, stop=(c + m < (i + 1) * P))
                t.matmul(big[0][:, i * P:(i + 1) * P], ident_b[:], mask_b[:],
                         start=False, stop=True).then_inc(s_s, 1)

            def batch(b, post, prep):
                pe.wait_ge(s_qk, b * 2 + 2)
                scores(b, 0)
                values()
                used = 0
                for n in range(TB):
                    i = ORDER[n]
                    pe.wait_ge(s_prob, b * TB + (n + 1))
                    first = used
                    for lo in range(0, i + 1, 4):
                        if used >= 2:
                            pe.wait_ge(s_probT, b * TURNS + (used - 1))
                        for j in range(lo, min(lo + 4, i + 1)):
                            m = t.transpose(turn[used % 2][:, (j - lo) * P:(j - lo + 1) * P],
                                            prob[:, n % 2, j * P:(j + 1) * P], ident[:])
                        m.then_inc(s_turn, 1)
                        used += 1
                    if n + 1 < TB:
                        scores(b, n + 1)
                    if n == 0:
                        pe.wait_ge(s_v, b + 1)
                    if n >= 2:
                        pe.wait_ge(s_x2, b * TB + (n - 1))
                    for j in range(i + 1):
                        if j % 4 == 0:
                            pe.wait_ge(s_probT, b * TURNS + (first + j // 4 + 1))
                        m = t.matmul(summ[n % 2][:, 0:P], probT[:, n % 2, j, :], v[:, j, :],
                                     start=(j == 0), stop=(j == i))
                    m.then_inc(s_att, 1)
                    if n == 0 and prep:
                        turn_normed(b + 1)
                    if n == 1 and post:
                        if prep:
                            pe.wait_ge(s_xnT, b + 2)
                        turn_normed2(b - 1)
                    if 2 <= n < 6 and prep:
                        if n == 2:
                            pe.wait_ge(s_xnT, b + 2)
                            if post:
                                pe.wait_ge(s_lo2, b)
                        else:
                            pe.wait_ge(s_rot, b * 4 + (n + 2))
                        project(n - 2, 1)
                    if n == 6 and post:
                        pe.wait_ge(s_hi2, b)
                        pe.wait_ge(s_lo2, b)
                        if prep:
                            pe.wait_ge(s_rot, b * 4 + 8)
                        logits(b - 1)
                if post:
                    pe.wait_ge(s_x2, b * TB + (TB - 1))
                    turn_logits(b - 1)

            turn_normed(0)
            pe.wait_ge(s_xnT, 1)
            project(0, 0)
            project(1, 1)
            pe.wait_ge(s_rot, 1)
            project(2, 0)
            pe.wait_ge(s_rot, 2)
            project(3, 1)
            batch(0, False, True)
            with nc.tensor.Fori(1, B - 1) as b:
                batch(b, True, True)
            batch(B - 1, True, False)
            turn_normed2(B - 1)
            pe.wait_ge(s_hi2, B)
            pe.wait_ge(s_lo2, B)
            logits(B - 1)
            turn_logits(B - 1)

            def split_products(out_ap, w, at, xs, first, last):
                for n, (ww, xx) in enumerate(((w_hi, xs[0]), (w_hi, xs[1]), (w_lo, xs[0]))):
                    m = t.matmul(out_ap, ww[:, w, at:at + P], xx, start=(first and n == 0), stop=(last and n == 2))
                return m

            def hidden(c, s, w, f, first=False):
                if not first:
                    pe.wait_ge(s_gelu, s * NF + (f + 1 - NF))
                at = bass.ds(c * CH, CH)
                split_products(hbank[f], w, f * P, (xT_hi[:, at], xT_lo[:, at]), True, True).then_inc(s_h, 1)

            def output(s, w, par, f):
                if f % 2 == 0:
                    pe.wait_ge(s_hilo, s * 2 + (f // 2 + 1))
                m = split_products(turn[par][:], w, F + f * P, (h_hi[:, par, f, :], h_lo[:, par, f, :]),
                                   f == 0, f == NF - 1)
                if f == NF - 1:
                    m.then_inc(s_y, 1)

            pe.wait_ge(s_wlo, 1)
            for f in range(NF):
                hidden(0, 0, 0, f, first=True)

            def count(n):
                pe.wait_ge(s_cnt, n)
                t.matmul(summ[1][:, 0:1], ones_b[:], count_b[:], start=True, stop=True).then_inc(s_tot, 1)

            with nc.tensor.Fori(0, NBIT // 10) as r:
                for j in range(2):
                    s, par = r * 2 + (1 + j), (1 + j) % 2
                    n = r * 10 + 5 * j
                    hidden(s, s, 0, 0)
                    count(n + 1)
                    for f in range(1, NF):
                        hidden(s, s, 0, f)
                    count(n + 2)
                    output(s - 1, 0, 1 - par, 0)
                    output(s - 1, 0, 1 - par, 1)
                    count(n + 3)
                    output(s - 1, 0, 1 - par, 2)
                    count(n + 4)
                    output(s - 1, 0, 1 - par, 3)
                    count(n + 5)
            for f in range(NF):
                hidden(NC - 1, NC - 1, 0, f)
            for f in range(NF):
                output(NC - 2, 0, 0, f)
            count(NBIT + 1)
            pe.wait_ge(s_cnt, NBIT + 2)
            t.matmul(summ[0][:, 0:E * NT], before_b[:], eq_b[:], start=True, stop=True)
            t.matmul(summ[0][:, E * NT:2 * E * NT], ones_b[:], eq_b[:], start=True, stop=True).then_inc(s_tot, 1)
            pe.wait_ge(s_gp, 1)
            for n in range(4):
                if n >= 2:
                    pe.wait_ge(s_gTc, n - 1)
                for i in range(NT // 4):
                    m = t.transpose(summ[n % 2][0:3 * E, :].bitcast(BF16)[:, i * P:(i + 1) * P],
                                    g_parts[:, n * (NT // 4) + i, :, :].rearrange("p a e -> p (a e)"), ident_b[:])
                m.then_inc(s_gt, 1)

            def position(e, c, s, w, par, w_before):
                for f in range(NF):
                    hidden(c, s, w, f)
                pe.wait_ge(s_gbc, s + (1 - NC))
                t.matmul(summ[0][:], pick_b[:, bass.ds(e - 1, 1), :].rearrange("p a m -> p (a m)"),
                         gT[:, bass.ds(c * CH, CH)], start=True, stop=True).then_inc(s_gbank, 1)
                for f in range(NF):
                    output(s - 1, w_before, 1 - par, f)

            def expert(e, w):
                pe.wait_ge(s_wlo, e + 1)
                position(e, 0, e * NC, w, 0, 1 - w)
                position(e, 1, e * NC + 1, w, 1, w)
                with nc.tensor.Fori(1, NC // 2) as cp:
                    for j in range(2):
                        position(e, cp * 2 + j, e * NC + (cp * 2 + j), w, j, w)

            with nc.tensor.Fori(0, E // 2) as ep:
                expert(ep * 2 + 1, 1)
                expert(ep * 2 + 2, 0)
            for f in range(NF):
                output(NE * NC - 1, 0, 1, f)
            for b in range(B):
                if b == 0:
                    pe.wait_ge(s_gelu, NE * NC * NF)
                pe.wait_ge(s_acc, 2 + NC * E + 2 * (b + 1))
                if b >= 2:
                    pe.wait_ge(s_res, b - 1)
                for i in range(TB):
                    m = t.transpose(big[b % 2][:, i * P:(i + 1) * P],
                                    outT[:, (b * TB + i) * P:(b * TB + i + 1) * P], ident[:])
                m.then_inc(s_fin, 1)

        @block.vector
        def _(dve):
            vec = nc.vector

            class Chain:

                def __init__(self, base):
                    self.base, self.n = base, 0

                def then(self, ins):
                    self.n += 1
                    ins.then_inc(s_dve, 1)
                    dve.wait_ge(s_dve, self.base + self.n)

            start = Chain(0)
            for n in range(NBIT):
                m = vec.memset(bit[:, n:n + 1], 1 << (NBIT - 1 - n))
            start.then(m)
            start.then(vec.memset(found[:], 0))
            dve.wait_ge(s_act0, 4)
            vec.tensor_tensor(gw_lo[:, 0:E], cols[:, ROWS_GW:NROWS], gw_hi[:, 0:E].bitcast(F32),
                              ALU.subtract).then_inc(s_gw, 1)

            def tile_of(b, i):
                return x2[:, bass.ds(b * TB + i, 1), :].rearrange("p a d -> p (a d)")

            NEWTON = 3 + 3 * 3

            def inverse_root(out, var, n, chain):
                w, y, z = nw[:, 0, 0:n], nw[:, 1, 0:n], nw[:, 2, 0:n]
                chain.then(vec.tensor_scalar(w, var, EPS, None, ALU.add))
                chain.then(vec.tensor_scalar(nwi[:, 0:n], w.bitcast(I32), 1, None, ALU.logical_shift_right))
                chain.then(vec.tensor_scalar(y.bitcast(I32), nwi[:, 0:n], -1.0, float(RSQRT_MAGIC), ALU.mult, ALU.add))
                for r in range(3):
                    chain.then(vec.tensor_tensor(z, y, w, ALU.mult))
                    chain.then(vec.scalar_tensor_tensor(z, z, -0.5, y, ALU.mult, ALU.mult))
                    if r < 2:
                        chain.then(vec.scalar_tensor_tensor(y, z, 1.5, y, ALU.add, ALU.mult))
                return vec.scalar_tensor_tensor(out, z, 1.5, y, ALU.add, ALU.mult)

            def statistics(tiles, chain):
                for i in tiles:
                    m = vec.bn_stats(stats[:, i, :], x2[:, i, :])
                chain.then(m)
                for i in tiles:
                    m = vec.bn_aggr(mv[:, i, :], stats[:, i, :])
                chain.then(m)

            def rotate(j, slot, n):
                dve.wait_ge(s_proj, n)
                vec.tensor_tensor((q_cos, q_sin, k_cos, k_sin)[j], big[slot][:], (costab, sintab)[j % 2][:],
                                  ALU.mult).then_inc(s_rot, 1)

            def add_key(b):
                dve.wait_ge(s_rot, b * 4 + 4)
                vec.tensor_tensor(k[:], k_cos, k_sin, ALU.add).then_inc(s_qk, 1)

            def row_max(b, n):
                i = ORDER[n]
                dve.wait_ge(s_s, b * TB + (n + 1))
                vec.tensor_reduce(neg_max[:, i:i + 1], big[0][:, 0:(i + 1) * P], AX.X, ALU.max,
                                  negate=True).then_inc(s_max, 1)

            def statistics2(b, chain):
                for i in range(TB):
                    m = vec.bn_aggr(mv2[:, i, :], stats2[:, i, :])
                chain.then(m)
                chain.then(inverse_root(inv2[:], mv2[:, :, 1], TB, chain))

            def scale1(b):
                for i in range(TB):
                    vec.tensor_scalar(xn[:, i, :], tile_of(b, i), mv[:, bass.ds(b * TB + i, 1), 0],
                                      inv1[:, bass.ds(b * TB + i, 1)], ALU.subtract, ALU.mult).then_inc(s_xn, 1)

            def scale2(b):
                for i in range(TB):
                    vec.tensor_scalar(xn2[:, i, :], tile_of(b, i), mv2[:, i, 0:1], inv2[:, i:i + 1],
                                      ALU.subtract, ALU.mult).then_inc(s_xn2, 1)

            def low_part(b):
                dve.wait_ge(s_xn2p, b + 1)
                dve.wait_ge(s_hi2, b + 1)
                at = bass.ds(b * T, T)
                vec.tensor_tensor(xT_lo[:, at], big[1][:], xT_hi[:, at].bitcast(F32), ALU.subtract).then_inc(s_lo2, 1)

            def logits_by_token(b):
                dve.wait_ge(s_lgT, b + 1)
                vec.tensor_copy(lg[:, :, bass.ds(b * TB, TB)],
                                summ[0][:, 256:256 + TB * E].rearrange("p (t e) -> p e t", e=E)).then_inc(s_lgc, 1)

            def batch(b, post, prep, chain):
                row_max(b, 0)
                if prep:
                    dve.wait_ge(s_xnp, b + 1)
                    scale1(b + 1)
                if post:
                    statistics2(b - 1, chain)
                for n in range(TB):
                    i = ORDER[n]
                    if n + 1 < TB:
                        row_max(b, n + 1)
                    if n == 0 and post:
                        scale2(b - 1)
                    if n == 2 and post:
                        low_part(b - 1)
                    if 3 <= n < 7 and prep:
                        rotate(n - 3, 1, b * 4 + (4 + n - 2))
                    if n == 7 and prep:
                        dve.wait_ge(s_s, b * TB + TB)
                        add_key(b + 1)
                    if n:
                        dve.wait_ge(s_x2, b * TB + n)
                    dve.wait_ge(s_prob, b * TB + (n + 1))
                    chain.then(vec.reciprocal(row_inv[:, i:i + 1], row_sum[:, i:i + 1]))
                    dve.wait_ge(s_att, b * TB + (n + 1))
                    vec.scalar_tensor_tensor(tile_of(b, i), summ[n % 2][:, 0:P], row_inv[:, i:i + 1],
                                             tile_of(b, i), ALU.mult, ALU.add).then_inc(s_x2, 1)
                    if n:
                        vec.bn_stats(stats2[:, ORDER[n - 1], :], tile_of(b, ORDER[n - 1]))
                dve.wait_ge(s_x2, b * TB + TB)
                vec.memset(nothing_v[:], 0.0)
                chain.then(vec.bn_stats(stats2[:, ORDER[TB - 1], :], tile_of(b, ORDER[TB - 1])))
                vec.memset(nothing_v[:], 0.0)
                if post:
                    logits_by_token(b - 1)

            dve.wait_ge(s_x, 16)
            statistics(range(TB), start)
            start.then(inverse_root(inv1[:, 0:TB], mv[:, 0:TB, 1], TB, start))
            scale1(0)
            dve.wait_ge(s_xr, 16)
            statistics(range(TB, NT), start)
            for j in range(4):
                rotate(j, j % 2, j + 1)
            add_key(0)
            m = inverse_root(inv1[:, TB:NT], mv[:, TB:NT, 1], NT - TB, start)
            start.then(m)
            batch(0, False, True, start)
            LINKS = 1 + NEWTON + TB + 1
            first = start.n
            with nc.vector.Fori(1, B - 1) as b:
                chain = Chain((b - 1) * LINKS + first)
                batch(b, True, True, chain)
                assert chain.n == LINKS, chain.n
            chain = Chain(first + LINKS * (B - 2))
            batch(B - 1, True, False, chain)
            statistics2(B - 1, chain)
            scale2(B - 1)
            low_part(B - 1)
            logits_by_token(B - 1)

            base = chain.base + chain.n

            def hi_part(s, par, half):
                dve.wait_ge(s_gelu, s * NF + (2 * half + 2))
                fs = slice(2 * half, 2 * half + 2)
                vec.tensor_copy(h_hi[:, par, fs, :], h[par][:, fs, :]).then_inc(s_hp, 1)

            def lo_part(s, par, half):
                dve.wait_ge(s_hp, s * 2 + (half + 1))
                fs = slice(2 * half, 2 * half + 2)
                vec.tensor_tensor(h_lo[:, par, fs, :], h[par][:, fs, :], h_hi[:, par, fs, :].bitcast(F32),
                                  ALU.subtract).then_inc(s_hilo, 1)

            def gate(s, e, par, slot):
                dve.wait_ge(s_y, s + 1)
                dve.wait_ge(s_acc, s + 1)
                vec.scalar_tensor_tensor(gated[:, par, :], turn[par][:], cols[:, bass.ds(ROWS_B2 + e, 1)],
                                         gate_bc[:, slot, :], ALU.add, ALU.mult).then_inc(s_gated, 1)

            chain = Chain(base)
            hi_part(0, 0, 0)
            hi_part(0, 0, 1)
            lo_part(0, 0, 0)
            lo_part(0, 0, 1)
            dve.wait_ge(s_lgc, B)
            by_token = "p e t -> p t e"

            def spread(v_):
                return v_.unsqueeze(1).to_broadcast([P, E, NT])

            chain.then(vec.tensor_reduce(rs[:, 0, :], lg[:].rearrange(by_token), AX.X, ALU.max))
            chain.then(vec.tensor_tensor(ra[:], lg[:], spread(rs[:, 0, :]), ALU.subtract))
            chain.then(vec.tensor_scalar(ra[:], ra[:], -100.0, None, ALU.max))
            chain.then(vec.tensor_scalar(rb[:], ra[:], LOG2E, ROUND, ALU.mult, ALU.add))
            chain.then(vec.tensor_scalar(rb[:], rb[:], ROUND, -127.0, ALU.subtract, ALU.max))
            chain.then(vec.tensor_scalar(pow2[:], rb[:], 127.0, 8388608.0, ALU.add, ALU.mult))
            chain.then(vec.scalar_tensor_tensor(ra[:], rb[:], -LN2_HI, ra[:], ALU.mult, ALU.add))
            chain.then(vec.scalar_tensor_tensor(ra[:], rb[:], -LN2_LO, ra[:], ALU.mult, ALU.add))
            fact = [1.0, 1.0, 2.0, 6.0, 24.0, 120.0, 720.0, 5040.0]
            chain.then(vec.tensor_scalar(rb[:], ra[:], 1.0 / fact[7], None, ALU.mult))
            for d in range(6, 0, -1):
                chain.then(vec.scalar_tensor_tensor(rb[:], rb[:], 1.0 / fact[d], ra[:], ALU.add, ALU.mult))
            chain.then(vec.scalar_tensor_tensor(rb[:], rb[:], 1.0, pow2[:].bitcast(F32), ALU.add, ALU.mult))
            chain.then(vec.tensor_reduce(rs[:, 0, :], rb[:].rearrange(by_token), AX.X, ALU.add))
            chain.then(vec.reciprocal(rs[:, 1, :], rs[:, 0, :]))
            chain.then(vec.tensor_tensor(lg[:], rb[:], spread(rs[:, 1, :]), ALU.mult))
            flat = "p e t -> p (e t)"
            scores, ra_ = lg[:].rearrange(flat), ra[:].rearrange(flat)

            def bit_try(n, chain):
                b_n = bit[:, bass.ds(n, 1)]
                chain.then(vec.tensor_tensor(cand[:], found[:], b_n, ALU.bitwise_or))
                vec.tensor_scalar(ra_, scores, cand[:].bitcast(F32), None, ALU.is_ge, ALU.add,
                                  accum_out=count_b[:]).then_inc(s_cnt, 1)

            def bit_keep(n, chain):
                dve.wait_ge(s_tot, n + 1)
                chain.then(vec.tensor_scalar(flag[:], summ[1][:, 0:1], float(K_TOP), bit[:, bass.ds(n, 1)],
                                             ALU.is_ge, ALU.mult))
                chain.then(vec.tensor_tensor(found[:], found[:], flag[:], ALU.bitwise_or))

            base += chain.n
            with nc.vector.Fori(0, NBIT // 10) as r:
                chain = Chain(r * 30 + base)
                for j in range(2):
                    s, par = r * 2 + (1 + j), (1 + j) % 2
                    for n, work in enumerate((hi_part, lo_part, hi_part, lo_part, None)):
                        bit_try(r * 10 + (5 * j + n), chain)
                        if work:
                            work(s, par, n // 2)
                        else:
                            gate(s - 1, 0, 1 - par, 1)
                        bit_keep(r * 10 + (5 * j + n), chain)
                assert chain.n == 30
            chain = Chain(base + 3 * NBIT)
            limit = found[:].bitcast(F32)
            vec.tensor_scalar(ra_, scores, limit, None, ALU.is_gt, ALU.add, accum_out=count_b[:]).then_inc(s_cnt, 1)
            vec.tensor_scalar(eq_b[:], scores, limit, None, ALU.is_equal).then_inc(s_cnt, 1)
            for half in range(2):
                hi_part(NC - 1, 1, half)
                lo_part(NC - 1, 1, half)
            gate(NC - 2, 0, 0, 1)
            dve.wait_ge(s_tot, NBIT + 2)
            before, inside = summ[0][:, 0:E * NT], summ[0][:, E * NT:2 * E * NT]
            chain.then(vec.tensor_tensor_scan(ra_, inside, zeros[:], 0.0, ALU.add, ALU.add))
            chain.then(vec.tensor_tensor(ra_, ra_, inside, ALU.subtract))
            chain.then(vec.tensor_tensor(ra_, ra_, before, ALU.add))
            chain.then(vec.tensor_copy(count_f[:, 0:1], summ[1][:, 0:1]))
            chain.then(vec.tensor_scalar(ra_, ra_, count_f[:, 0:1], float(K_TOP), ALU.add, ALU.is_lt))
            chain.then(vec.tensor_tensor(ra_, ra_, eq_b[:], ALU.mult))
            chain.then(vec.scalar_tensor_tensor(ra_, scores, limit, ra_, ALU.is_gt, ALU.add))
            chain.then(vec.tensor_tensor(ra_, ra_, scores, ALU.mult))
            part = [g_parts[:, :, n, :].rearrange("p t e -> p e t") for n in range(3)]
            chain.then(vec.tensor_copy(part[0], ra[:]))
            chain.then(vec.tensor_tensor(rb[:], ra[:], part[0], ALU.subtract))
            chain.then(vec.tensor_copy(part[1], rb[:]))
            chain.then(vec.tensor_tensor(ra[:], rb[:], part[1], ALU.subtract))
            vec.tensor_copy(part[2], ra[:]).then_inc(s_gp, 1)
            for n in range(4):
                dve.wait_ge(s_gt, n + 1)
                m = vec.tensor_copy(gT[0:3 * E, n * (S // 4):(n + 1) * (S // 4)],
                                    summ[n % 2][0:3 * E, :].bitcast(BF16))
                m.then_inc(s_gTc, 1)
            dve.wait_ge(s_gTc, 4)
            vec.tensor_copy(count_f[:, 1:2], count_f[:, 0:1]).then_inc(s_gbc, 1)

            def position(e, s, par, first):
                for half in range(2):
                    hi_part(s, par, half)
                    lo_part(s, par, half)
                if not first:
                    dve.wait_ge(s_gbc, s + (1 - NC))
                    gate(s - 1, e, 1 - par, 1 - par)
                else:
                    dve.wait_ge(s_gbc, s + (1 - NC))
                    gate(s - 1, e - 1, 1 - par, 1 - par)

            def expert(e):
                position(e, e * NC, 0, True)
                position(e, e * NC + 1, 1, False)
                with nc.vector.Fori(1, NC // 2) as cp:
                    for j in range(2):
                        position(e, e * NC + (cp * 2 + j), j, False)

            with nc.vector.Fori(0, E // 2) as ep:
                expert(ep * 2 + 1)
                expert(ep * 2 + 2)
            dve.wait_ge(s_gbc, NE * NC + (1 - NC))
            gate(NE * NC - 1, E, 1, 1)
            for b in range(B):
                dve.wait_ge(s_fin, b + 1)
                o = x2[:, b * TB:(b + 1) * TB, :].rearrange("p t d -> p (t d)")
                vec.tensor_tensor(o, o, big[b % 2][:], ALU.add).then_inc(s_res, 1)


def rotation_tables(T, D, base=10000.0):
    import numpy as np
    half = D // 2
    freqs = np.power(np.float32(base), -np.arange(half, dtype=np.float32) / np.float32(half)).astype(np.float32)
    angles = (freqs[:, None] * np.arange(T, dtype=np.float32)[None, :]).astype(np.float32)
    cos, sin = np.cos(angles).astype(np.float32), np.sin(angles).astype(np.float32)
    return np.concatenate([cos, cos]), np.concatenate([-sin, sin])


_INS = ['L0_attn_x', 'L0_attn_wq', 'L0_attn_wk', 'L0_attn_wv', 'L0_attn_wo', 'L0_ffn_gate_weight', 'L0_ffn_W1',
        'L0_ffn_b1', 'L0_ffn_W2', 'L0_ffn_b2', 'L0_ffn_Ws1', 'L0_ffn_bs1', 'L0_ffn_Ws2', 'L0_ffn_bs2']


def kernel(**inputs):
    import numpy as np
    import concourse.bacc as bacc
    from concourse.bass_utils import run_bass_kernel_spmd

    nc = bacc.Bacc("TRN2", target_bir_lowering=False, num_devices=1)
    arrays = {name: np.ascontiguousarray(inputs[name]) for name in _INS}
    B, T, D = arrays['L0_attn_x'].shape
    arrays['cos'], arrays['sin'] = rotation_tables(T, D)
    args = [nc.dram_tensor(name, a.shape, mybir.dt.from_np(a.dtype), kind="ExternalInput").ap()
            for name, a in arrays.items()]
    args.append(nc.dram_tensor("out", (B, T, D), F32, kind="ExternalOutput").ap())
    moe_layer(nc, *args)
    r = run_bass_kernel_spmd(nc, [arrays], core_ids=[0])
    return r.results[0]["out"]
```

```python
from contextlib import ExitStack

import concourse.bass as bass
from concourse import mybir

ALU = mybir.AluOpType
ACT = mybir.ActivationFunctionType
AX = mybir.AxisListType
F32 = mybir.dt.float32
F32R = mybir.dt.float32r
BF16 = mybir.dt.bfloat16
I32 = mybir.dt.int32

P = 128
EPS = 1e-5
MASKED = -1e30
LOG2E = 1.4426950408889634
LN2_HI = 0.693359375
LN2_LO = -2.12194440e-4
ROUND = 12582912.0
RSQRT_MAGIC = 0x5F3759DF


def moe_layer(nc, x_in, wq_in, wk_in, wv_in, wo_in, gate_in, W1_in, b1_in, W2_in, b2_in,
              Ws1_in, bs1_in, Ws2_in, bs2_in, cos_in, sin_in, out, gate_rows):
    B, T, D = x_in.shape
    E, _, F = W1_in.shape
    assert D == P and F % P == 0 and T % 512 == 0
    TB = T // P
    NT = B * TB
    S = B * T
    NF = F // P
    K_TOP = 2 * S
    CH = 512
    NC = S // CH
    NE = E + 1
    QK_SCALE = 1.0 / D
    NBIT = 30
    BITS = 4
    LEAD = 4
    LATE = 4
    DIRECT = NC + LATE
    EARLY = DIRECT + 2
    LAST_BITS = NBIT - BITS * (NC - LEAD + LATE - 1)
    assert NC == 8 and E % 2 == 0 and TB == 8 and 0 < LAST_BITS <= BITS

    ORDER = list(range(TB - 1, TB // 2 - 1, -1)) + [0, 3, 1, 2]
    TURNS = sum((i + 4) // 4 for i in range(TB))

    ROWS_B1, ROWS_B2, ROWS_GW = 0, NE * NF, NE * NF + NE
    NROWS = ROWS_GW + E

    with ExitStack() as ctx:
        def sb(name, shape, dt):
            return ctx.enter_context(nc.sbuf_tensor(name, shape, dt))

        def pb(name, shape, dt):
            return ctx.enter_context(nc.psum_tensor(name, shape, dt))

        def sem(name):
            return ctx.enter_context(nc.semaphore(name))

        ident = sb("ident", [P, P], F32)
        ident_b = sb("ident_b", [P, P], BF16)
        mask_b = sb("mask_b", [P, P], BF16)
        before_b = sb("before_b", [P, P], BF16)
        ones_b = sb("ones_b", [P, P], BF16)
        work = sb("work", [P, 4, T], F32)
        costab, sintab = work[:, 2, :], work[:, 3, :]
        wqk = sb("wqk", [P, 2, D], F32)
        w4 = sb("w4", [P, 4, D], F32)
        wvo = sb("wvo", [P, 3, D], F32)
        wp = sb("wp", [P, D], F32)
        rows = sb("rows", [NROWS, P], F32)
        cols = sb("cols", [P, NROWS], F32)
        gw_hi = sb("gw_hi", [P, P], F32R)
        gw_lo = sb("gw_lo", [P, P], F32R)
        x2 = sb("x2", [P, NT, D], F32)
        xn, xn2 = (work[:, n, :].rearrange("p (t d) -> p t d", d=D) for n in range(2))
        xnT = sb("xnT", [P, T], F32)
        qk = sb("qk", [P, 2, T], F32)
        q, k = qk[:, 0, :], qk[:, 1, :]
        v = sb("v", [P, TB, D], F32)
        raw = sb("raw", [P, 2, T], F32)
        prob = sb("prob", [P, 2, T], F32)
        probT = sb("probT", [P, 2, TB, P], F32)
        neg_max = sb("neg_max", [P, TB], F32)
        row_sum = sb("row_sum", [P, TB], F32)
        row_inv = sb("row_inv", [P, TB], F32)
        stats = sb("stats", [P, NT, 6], F32)
        mv = sb("mv", [P, NT, 2], F32)
        stats2 = sb("stats2", [P, TB, 6], F32)
        mv2 = sb("mv2", [P, TB, 2], F32)
        inv1 = sb("inv1", [P, NT], F32)
        inv2 = sb("inv2", [P, TB], F32)
        nw = sb("nw", [P, 3, NT], F32)
        nwi = sb("nwi", [P, NT], I32)
        xT_hi = sb("xT_hi", [P, S], F32R)
        xT_lo = sb("xT_lo", [P, S], F32R)
        lg = sb("lg", [P, E, NT], F32)
        ra = sb("ra", [P, E, NT], F32)
        rb = sb("rb", [P, E, NT], F32)
        pow2 = sb("pow2", [P, E, NT], I32)
        rs = sb("rs", [P, 2, NT], F32)
        bit = sb("bit", [P, 32], I32)
        cand = sb("cand", [P, 1], I32)
        cand_next = sb("cand_next", [P, 1], I32)
        flag = sb("flag", [P, 1], I32)
        count_b = sb("count_b", [P, 1], BF16)
        count_f = sb("count_f", [P, 2], F32)
        eq_b = sb("eq_b", [P, E * NT], BF16)
        zeros = sb("zeros", [P, E * NT], F32)
        g_rows = sb("g_rows", [P, E * NT // P, P], F32)
        lgT = sb("lgT", [P, T], F32)
        w_raw = sb("w_raw", [P, 2, 2 * F], F32)
        w_hi = sb("w_hi", [P, 2, 2 * F], F32R)
        w_lo = sb("w_lo", [P, 2, 2 * F], F32R)
        h = [prob[:].rearrange("p a (f c) -> p (a f) c", c=CH), probT[:].rearrange("p a (f t) c -> p (a f) (t c)", f=2)]
        h_hi = sb("h_hi", [P, 2, NF, CH], F32R)
        h_lo = sb("h_lo", [P, 2, NF, CH], F32R)
        bias_now = sb("bias_now", [P, 2, NF], F32)
        gate_bc = work[:].rearrange("p n t -> p (n t)")
        nothing_v = sb("nothing_v", [P, 1], F32)
        gated = sb("gated", [P, 2, CH], F32)
        outT = sb("outT", [P, S], F32)

        late = qk[:].rearrange("p a (s c) -> p (a s) c", c=CH)

        q_cos, q_sin, k_cos, k_sin = (outT[:, n * T:(n + 1) * T] for n in range(4))

        big = [pb(f"big{i}", [P, 1024], F32) for i in range(2)]
        turn = [pb(f"turn{i}", [P, 512], F32) for i in range(2)]
        summ = [pb(f"summ{i}", [P, 512], F32) for i in range(2)]
        hbank = [big[f // 2][:, (f % 2) * 512:(f % 2) * 512 + 512] for f in range(NF)]

        s_wqk = sem("query_key_weights_loaded")
        s_wvo = sem("value_output_weights_loaded")
        s_trig = sem("rotation_tables_loaded")
        s_rows = sem("small_vectors_loaded")
        s_ident = sem("identity_ready")
        s_w4 = sem("key_weights_ready")
        s_x = sem("x_loaded")
        s_const = sem("constants_ready")
        s_pe0 = sem("setup_products_done")
        s_act0 = sem("setup_copies_done")
        s_xr = sem("x_of_later_batches_loaded")
        s_xn = sem("normed1_ready")
        s_xn2 = sem("normed2_ready")
        s_xnp = sem("normed1_turned")
        s_xnT = sem("normed1_turned_copied")
        s_xn2p = sem("normed2_turned")
        s_proj = sem("projection_summed")
        s_vp = sem("values_summed")
        s_lgp = sem("logits_summed")
        s_s = sem("scores_summed")
        s_rot = sem("rotation_part_ready")
        s_rawc = sem("query_or_key_copied")
        s_swap = [sem("query_halves_swapped"), sem("key_halves_swapped")]
        s_sin = sem("sine_part_ready")
        s_qk = sem("query_or_key_ready")
        s_v = sem("values_ready")
        s_max = sem("row_max_ready")
        s_prob = sem("probs_ready")
        s_turn = sem("probs_turned")
        s_probT = sem("turned_probs_copied")
        s_att = sem("attention_tile_summed")
        s_x2 = sem("attention_added")
        s_hi2 = sem("normed2_hi_ready")
        s_lo2 = sem("normed2_lo_ready")
        s_lg = sem("logits_copied")
        s_lgT = sem("logits_turned")
        s_lgc = sem("logits_by_token_ready")
        s_gw = sem("gate_weight_ready")
        s_raw = sem("expert_weights_loaded")
        s_whi = sem("expert_weights_hi_ready")
        s_wlo = sem("expert_weights_lo_ready")
        s_bias = sem("expert_bias_copied")
        s_h = sem("hidden_chunk_summed")
        s_gelu = sem("gelu_chunk_ready")
        s_hp = sem("hidden_hi_ready")
        s_hilo = sem("hidden_split_ready")
        s_y = sem("expert_step_summed")
        s_gout = sem("gate_rows_stored")
        s_gbc = sem("gates_of_two_steps_loaded")
        s_lmul = sem("late_step_gated")
        s_gated = sem("expert_step_gated_or_kept")
        s_acc = sem("expert_step_added")
        s_cnt = sem("count_ready")
        s_tot = sem("count_summed")
        s_gp = sem("gates_ready")
        s_gt = sem("gates_turned")
        s_gTc = sem("gate_rows_ready")
        s_fin = sem("result_turned")
        s_res = sem("result_added")
        s_out = sem("result_stored")
        s_dve = sem("vector_chain")
        s_pool0 = sem("pool_chain")

        block = ctx.enter_context(nc.Block())

        @block.sync
        def _(sp):
            sp.dma_start(x2[:, 0:TB, :], x_in[0, :, :].rearrange("(t p) d -> p t d", p=P)).then_inc(s_x, 16)
            sp.dma_start(costab, cos_in).then_inc(s_trig, 16)
            sp.dma_start(sintab, sin_in).then_inc(s_trig, 16)
            sp.dma_start(x2[:, TB:NT, :],
                         x_in[1:B, :, :].rearrange("b (t p) d -> p (b t) d", p=P)).then_inc(s_xr, 16)
            sp.dma_start(rows[ROWS_B1:ROWS_B1 + NF, :], bs1_in.rearrange("(c p) -> c p", p=P)).then_inc(s_rows, 16)
            sp.dma_start(rows[ROWS_B1 + NF:ROWS_B2, :], b1_in.rearrange("e (c p) -> (e c) p", p=P)).then_inc(s_rows, 16)
            sp.dma_start(rows[ROWS_B2:ROWS_B2 + 1, :], bs2_in.rearrange("(a p) -> a p", a=1)).then_inc(s_rows, 16)
            sp.dma_start(rows[ROWS_B2 + 1:ROWS_GW, :], b2_in).then_inc(s_rows, 16)
            sp.dma_start(rows[ROWS_GW:NROWS, :], gate_in).then_inc(s_rows, 16)

            def load_expert(par, w1, w2):
                sp.dma_start(w_raw[:, par, 0:F], w1).then_inc(s_raw, 16)
                sp.dma_start(w_raw[:, par, F:2 * F].rearrange("p (c d) -> p c d", d=D), w2).then_inc(s_raw, 16)

            def w1_of(e):
                return W1_in[bass.ds(e, 1), :, :].rearrange("a d f -> d (a f)")

            def w2_of(e):
                return W2_in[bass.ds(e, 1), :, :].rearrange("a (c p) d -> p (a c) d", p=P)

            load_expert(0, Ws1_in, Ws2_in.rearrange("(c p) d -> p c d", p=P))
            sp.wait_ge(s_raw, 32)
            load_expert(1, w1_of(0), w2_of(0))
            H = D // 2
            with nc.sync.Fori(0, B - 1) as b:
                for j, swapped in ((0, q_sin), (1, k_sin)):
                    sp.wait_ge(s_rawc, b * 2 + (j + 1))
                    sp.dma_start(swapped[0:H, :], raw[H:D, j, :]).then_inc(s_swap[j], 16)
                    sp.dma_start(swapped[H:D, :], raw[0:H, j, :]).then_inc(s_swap[j], 16)
            sp.wait_ge(s_wlo, 2)
            load_expert(0, w1_of(1), w2_of(1))

            sp.wait_ge(s_gTc, 1)
            sp.dma_start(gate_rows.rearrange("e (t p) -> (e t) p", p=P).rearrange("(n r) p -> r n p", r=P),
                         g_rows[:]).then_inc(s_gout, 16)
            sp.wait_ge(s_gout, 16)

            def load_gates(e, cp):
                sp.dma_start(gate_bc[:, cp * 2 * CH:(cp + 1) * 2 * CH],
                             gate_rows[bass.ds(e - 1, 1), cp * 2 * CH:(cp + 1) * 2 * CH].to_broadcast([P, 2 * CH])
                             ).then_inc(s_gbc, 16)

            for n, cp in enumerate((2, 3, 0, 1)):
                if n:
                    sp.wait_ge(s_gbc, 16 * n)
                load_gates(1, cp)

            def load(e, next_par):
                if next_par is not None:
                    sp.wait_ge(s_wlo, e + 1)
                    load_expert(next_par, w1_of(e), w2_of(e))
                for cp in range(NC // 2):
                    sp.wait_ge(s_gated, e * NC + (2 * cp - 1))
                    load_gates(e, cp)

            sp.wait_ge(s_wlo, 3)
            load_expert(1, w1_of(2), w2_of(2))
            for cp in range(2):
                sp.wait_ge(s_gated, 2 * NC + (2 * cp - 1))
                sp.wait_ge(s_lmul, LATE)
                load_gates(2, cp)
            for cp in range(2, NC // 2):
                sp.wait_ge(s_gated, 2 * NC + (2 * cp - 1))
                load_gates(2, cp)
            with nc.sync.Fori(1, E // 2 - 1) as ep:
                load(ep * 2 + 1, 0)
                load(ep * 2 + 2, 1)
            load(E - 1, 0)
            load(E, None)
            for c in range(NC):
                sp.wait_ge(s_res, c + 1 if c < NC - 2 else c + 2)
                tiles = slice(c * CH // P, (c + 1) * CH // P)
                sp.dma_start(out.rearrange("b (t p) d -> p (b t) d", p=P)[:, tiles, :],
                             x2[:, tiles, :]).then_inc(s_out, 16)
            sp.wait_ge(s_out, 16 * NC)

        @block.gpsimd
        def _(pool):
            g = nc.gpsimd
            n = [0]

            def then(ins):
                n[0] += 1
                ins.then_inc(s_pool0, 1)
                pool.wait_ge(s_pool0, n[0])

            then(g.memset(ident[:], 0.0))
            then(g.affine_select(out=ident[:], in_=ident[:], compare_op=ALU.not_equal, fill=1.0, base=0,
                                 pattern=[[-1, P]], channel_multiplier=1))
            g.tensor_copy(ident_b[:], ident[:]).then_inc(s_ident, 1)
            then(g.memset(mask_b[:], 0.0))
            g.affine_select(out=mask_b[:], in_=mask_b[:], compare_op=ALU.is_ge, fill=MASKED, base=0,
                            pattern=[[-1, P]], channel_multiplier=1).then_inc(s_const, 1)
            g.memset(gw_hi[:].bitcast(F32), 0.0).then_inc(s_const, 1)
            g.memset(gw_lo[:].bitcast(F32), 0.0).then_inc(s_const, 1)
            g.memset(ones_b[:], 1.0).then_inc(s_const, 1)
            then(g.memset(before_b[:], 0.0))
            g.affine_select(out=before_b[:], in_=before_b[:], compare_op=ALU.is_ge, fill=1.0, base=0,
                            pattern=[[-1, P]], channel_multiplier=1).then_inc(s_const, 1)
            g.memset(zeros[:], 0.0).then_inc(s_const, 1)

            pool.wait_ge(s_rot, 2)
            g.tensor_tensor(q, q_cos, q_sin, ALU.add).then_inc(s_qk, 1)
            with nc.gpsimd.Fori(1, B) as b:
                for j, cos_part, sin_part in ((0, q_cos, q_sin), (1, k_cos, k_sin)):
                    pool.wait_ge(s_rawc, b * 2 + (j - 1))
                    g.tensor_tensor(cos_part, raw[:, j, :], costab, ALU.mult).then_inc(s_rot, 1)
                    pool.wait_ge(s_swap[j], b * 32)
                    g.tensor_tensor(sin_part, sin_part, sintab, ALU.mult).then_inc(s_sin, 1)
                pool.wait_ge(s_sin, b * 2)
                pool.wait_ge(s_rot, b * 2 + 3)
                pool.wait_ge(s_s, b * TB)
                g.tensor_tensor(q, q_cos, q_sin, ALU.add).then_inc(s_qk, 1)
            pool.wait_ge(s_qk, 2 * B)
            for half in range(2):
                g.memset(outT[:, half * (S // 2):(half + 1) * (S // 2)], 0.0).then_inc(s_acc, 1)

            def split_weights(par, n_whi):
                pool.wait_ge(s_whi, n_whi)
                g.tensor_tensor(w_lo[:, par, :], w_raw[:, par, :], w_hi[:, par, :].bitcast(F32),
                                ALU.subtract).then_inc(s_wlo, 1)

            def accumulate(done, c, par):
                pool.wait_ge(s_gated, done + 1)
                o = outT[:, bass.ds(c * CH, CH)]
                g.tensor_tensor(o, o, gated[:, par, :], ALU.add).then_inc(s_acc, 1)

            def lo_parts(s, par):
                for half in range(2):
                    pool.wait_ge(s_gelu, s * NF + (2 * half + 2))
                    fs = slice(2 * half, 2 * half + 2)
                    g.tensor_tensor(h_lo[:, par, fs, :], h[par][:, fs, :], h_hi[:, par, fs, :].bitcast(F32),
                                    ALU.subtract).then_inc(s_hilo, 1)

            split_weights(0, 1)
            lo_parts(0, 0)
            lo_parts(1, 1)
            pool.wait_ge(s_acc, 2)
            with nc.gpsimd.Fori(1, NC // 2) as cp:
                for j in range(2):
                    lo_parts(cp * 2 + j, j)
                    accumulate(cp * 2 + (j - 2), cp * 2 + (j - 2), j)
            for s in (NC, NC + 1):
                lo_parts(s, s % 2)
                accumulate(s - 2, s - 2, s % 2)
            for s in range(NC + 2, DIRECT):
                lo_parts(s, s % 2)
            pool.wait_ge(s_wlo, 2)
            split_weights(0, 3)
            for s in range(DIRECT, EARLY):
                lo_parts(s, s % 2)

            def accumulate_late(c):
                pool.wait_ge(s_gbc, 16 * (c // 2 + 3))
                pool.wait_ge(s_gated, NC + c + 1)
                g.tensor_tensor(late[:, c, :], late[:, c, :], gate_bc[:, c * CH:(c + 1) * CH],
                                ALU.mult).then_inc(s_lmul, 1)
                pool.wait_ge(s_lmul, c + 1)
                o = outT[:, c * CH:(c + 1) * CH]
                g.tensor_tensor(o, o, late[:, c, :], ALU.add).then_inc(s_acc, 1)

            accumulate(DIRECT, LATE, 0)
            accumulate(DIRECT + 1, LATE + 1, 1)
            accumulate_late(0)
            accumulate_late(1)
            accumulate(EARLY, LATE + 2, 0)
            accumulate_late(2)
            accumulate(EARLY + 1, LATE + 3, 1)
            accumulate_late(3)

            def expert(e, par, split):
                for j in range(2):
                    accumulate(e * NC + j, j, j)
                if split:
                    split_weights(1 - par, e + 2)
                with nc.gpsimd.Fori(1, NC // 2) as cp:
                    for j in range(2):
                        accumulate(e * NC + (cp * 2 + j), cp * 2 + j, j)

            expert(2, 0, True)
            with nc.gpsimd.Fori(1, E // 2 - 1) as ep:
                expert(ep * 2 + 1, 1, True)
                expert(ep * 2 + 2, 0, True)
            expert(E - 1, 1, True)
            for c in range(NC - 1):
                accumulate(E * NC + c, c, c % 2)

        @block.scalar
        def _(act):
            a = nc.scalar
            H = D // 2
            act.dma_start(wqk[:, 0, :], wq_in.rearrange("h m d -> m (h d)")).then_inc(s_wqk, 16)
            act.dma_start(wqk[:, 1, :], wk_in.rearrange("h m d -> m (h d)")).then_inc(s_wqk, 16)
            act.dma_start(wvo[:, 0, :], wv_in.rearrange("h m d -> m (h d)")).then_inc(s_wvo, 16)
            act.dma_start(wvo[:, 2, :], wo_in.rearrange("h d m -> d (h m)")).then_inc(s_wvo, 16)
            act.wait_ge(s_wqk, 32)
            a.mul(w4[:, 0, :], wqk[:, 0, :], QK_SCALE)
            a.mul(w4[:, 1, 0:H], wqk[:, 0, H:D], QK_SCALE)
            a.mul(w4[:, 1, H:D], wqk[:, 0, 0:H], QK_SCALE).then_inc(s_act0, 1)

            def split_weights(par, n_raw):
                act.wait_ge(s_raw, n_raw)
                a.copy(w_hi[:, par, :], w_raw[:, par, :]).then_inc(s_whi, 1)

            def turn_copy(b):
                act.wait_ge(s_xnp, b + 1)
                a.copy(xnT[:], big[1][:]).then_inc(s_xnT, 1)

            def hi_copy(b):
                act.wait_ge(s_xn2p, b + 1)
                a.copy(xT_hi[:, bass.ds(b * T, T)], big[1][:]).then_inc(s_hi2, 1)

            def logits_copy(b, c):
                act.wait_ge(s_lgp, b * 2 + (c + 1))
                return a.copy(lgT[:, c * 512:(c + 1) * 512], big[1][:, c * 512:(c + 1) * 512])

            def exps(b, n):
                i = ORDER[n]
                act.wait_ge(s_max, b * TB + (n + 1))
                a.activation(prob[:, n % 2, 0:(i + 1) * P], big[0][:, 0:(i + 1) * P], ACT.Exp,
                             bias=neg_max[:, i:i + 1], accum_out=row_sum[:, i:i + 1]).then_inc(s_prob, 1)

            def raw_copy(b, j):
                act.wait_ge(s_proj, b * 2 + (3 + j))
                a.copy(raw[:, j, :], big[1][:]).then_inc(s_rawc, 1)

            def batch(b, post, prep):
                exps(b, 0)
                act.wait_ge(s_vp, b + 1)
                a.copy(v[:].rearrange("p t d -> p (t d)"), big[1][:]).then_inc(s_v, 1)
                used = 0
                for n in range(TB):
                    i = ORDER[n]
                    if n == 2 and prep:
                        if post:
                            act.wait_ge(s_swap[0], b * 32)
                            act.wait_ge(s_rot, b * 2 + 3)
                        raw_copy(b + 1, 0)
                    if n >= 2:
                        act.wait_ge(s_att, b * TB + (n - 1))
                    for lo in range(0, i + 1, 4):
                        m = min(4, i + 1 - lo)
                        act.wait_ge(s_turn, b * TURNS + (used + 1))
                        a.copy(probT[:, n % 2, lo:lo + m, :].rearrange("p t c -> p (t c)"),
                               turn[used % 2][:, 0:m * P]).then_inc(s_probT, 1)
                        used += 1
                    if n == 4 and prep:
                        if post:
                            act.wait_ge(s_swap[1], b * 32)
                            act.wait_ge(s_rot, b * 2 + 4)
                        raw_copy(b + 1, 1)
                    if n + 1 < TB:
                        exps(b, n + 1)
                    if n == 6 and post:
                        logits_copy(b - 1, 0)
                    if n == 0 and prep:
                        turn_copy(b + 1)
                    if n == 4 and post:
                        hi_copy(b - 1)
                    if n == 7 and post:
                        logits_copy(b - 1, 1).then_inc(s_lg, 1)
                    if n in (3, 5) and not prep:
                        split_weights(n // 5, 32 * (n // 5 + 1))

            turn_copy(0)
            act.wait_ge(s_pe0, 1)
            a.copy(wvo[:, 1, :], turn[0][:, 0:P]).then_inc(s_act0, 1)
            act.wait_ge(s_pe0, 2)
            a.copy(wp[:], turn[0][:, 0:P]).then_inc(s_act0, 1)
            act.wait_ge(s_pe0, 3)
            a.copy(cols[:], turn[1][:, 0:NROWS]).then_inc(s_act0, 1)
            act.wait_ge(s_act0, 4)
            act.wait_ge(s_const, 3)
            a.copy(gw_hi[:, 0:E], cols[:, ROWS_GW:NROWS]).then_inc(s_act0, 1)
            batch(0, False, True)
            with nc.scalar.Fori(1, B - 1) as b:
                batch(b, True, True)
            batch(B - 1, True, False)

            def gelu_twice(s, par, bias, fs=range(NF), after=True):
                for f in fs:
                    if after:
                        act.wait_ge(s_hilo, s * 2 + (f // 2 - 3))
                    act.wait_ge(s_h, s * NF + (f + 1))
                    a.activation(h[par][:, f, :], hbank[f], ACT.Gelu_apprx_tanh, bias=bias[:, f:f + 1])
                    a.activation(h_hi[:, par, f, :], hbank[f], ACT.Gelu_apprx_tanh,
                                 bias=bias[:, f:f + 1]).then_inc(s_gelu, 1)

            shared_bias = cols[:, 0:NF]
            gelu_twice(0, 0, shared_bias, after=False)
            gelu_twice(1, 1, shared_bias, range(0, 2), after=False)
            for c in range(2):
                act.wait_ge(s_xn2p, B + c)
                at = (B - 1) * T + c * 512
                a.copy(xT_hi[:, at:at + 512], summ[c][:]).then_inc(s_hi2, 1)
            gelu_twice(1, 1, shared_bias, range(2, 4), after=False)
            for c in range(2):
                act.wait_ge(s_lgp, 2 * (B - 1) + c + 1)
                a.copy(lgT[:, c * 512:(c + 1) * 512], summ[c][:]).then_inc(s_lg, 1)
            gelu_twice(2, 0, shared_bias)
            gelu_twice(3, 1, shared_bias)
            with nc.scalar.Fori(0, (NC - LEAD) // 2) as r:
                for j in range(2):
                    gelu_twice(r * 2 + (LEAD + j), j, shared_bias)

            bias = bias_now[:, 1, :]
            a.copy(bias, cols[:, NF:2 * NF]).then_inc(s_bias, 1)
            act.wait_ge(s_bias, 1)
            for s in range(NC, NC + 3):
                gelu_twice(s, s % 2, bias)
            act.wait_ge(s_y, NC)
            split_weights(0, 96)
            for s in range(NC + 3, EARLY):
                gelu_twice(s, s % 2, bias)

            def gelu(s, par, bias, fs=range(NF)):
                for f in fs:
                    act.wait_ge(s_h, s * NF + (f + 1))
                    act.wait_ge(s_hilo, s * 2 + (f // 2 - 3))
                    a.activation(h[par][:, f, :], hbank[f], ACT.Gelu_apprx_tanh,
                                 bias=bias[:, f:f + 1]).then_inc(s_gelu, 1)

            gelu(EARLY, 0, bias)
            gelu(EARLY + 1, 1, bias)

            def expert(e, par, split):
                bias = bias_now[:, par, :]
                a.copy(bias, cols[:, bass.ds(e * NF, NF)]).then_inc(s_bias, 1)
                act.wait_ge(s_bias, e)
                gelu(e * NC, 0, bias)
                gelu(e * NC + 1, 1, bias)
                if split:
                    act.wait_ge(s_y, e * NC)
                    split_weights(1 - par, e * 32 + 64)
                with nc.scalar.Fori(1, NC // 2) as cp:
                    for j in range(2):
                        gelu(e * NC + (cp * 2 + j), j, bias)

            expert(2, 0, True)
            with nc.scalar.Fori(1, E // 2 - 1) as ep:
                expert(ep * 2 + 1, 1, True)
                expert(ep * 2 + 2, 0, True)
            expert(E - 1, 1, True)
            expert(E, 0, False)

        @block.tensor
        def _(pe):
            t = nc.tensor

            def turn_normed(b):
                for i in range(TB):
                    pe.wait_ge(s_xn, b * TB + (i + 1))
                    m = t.transpose(big[1][:, i * P:(i + 1) * P], xn[:, i, :], ident[:])
                m.then_inc(s_xnp, 1)

            def turn_normed2(b):
                for i in range(TB):
                    pe.wait_ge(s_xn2, b * TB + (i + 1))
                    m = t.transpose(big[1][:, i * P:(i + 1) * P], xn2[:, i, :], ident[:])
                m.then_inc(s_xn2p, 1)

            def project(w, slot):
                for c in range(T // 512):
                    m = t.matmul(big[slot][:, c * 512:(c + 1) * 512], w4[:, w, :],
                                 xnT[:, c * 512:(c + 1) * 512], start=True, stop=True)
                m.then_inc(s_proj, 1)

            def values():
                for i in range(TB):
                    m = t.matmul(big[1][:, i * P:(i + 1) * P], xnT[:, i * P:(i + 1) * P], wp[:],
                                 start=True, stop=True)
                m.then_inc(s_vp, 1)

            def logits(b, chunks):
                for c in chunks:
                    at = bass.ds(b * T + c * 512, 512)
                    for n, (gg, xx) in enumerate(((gw_hi, xT_hi), (gw_hi, xT_lo), (gw_lo, xT_hi))):
                        m = t.matmul(big[1][:, c * 512:(c + 1) * 512], gg[:], xx[:, at],
                                     start=(n == 0), stop=(n == 2))
                m.then_inc(s_lgp, 1)

            def turn_logits(b):
                for i in range(TB):
                    m = t.matmul(summ[0][:, 256 + i * E:256 + (i + 1) * E], lgT[:, i * P:(i + 1) * P],
                                 ident[:, 0:E], start=True, stop=True)
                m.then_inc(s_lgT, 1)

            def scores(b, n):
                i = ORDER[n]
                for c in range(0, (i + 1) * P, 512):
                    m = min(512, (i + 1) * P - c)
                    t.matmul(big[0][:, c:c + m], q[:, i * P:(i + 1) * P], k[:, c:c + m],
                             start=True, stop=(c + m < (i + 1) * P))
                t.matmul(big[0][:, i * P:(i + 1) * P], ident_b[:], mask_b[:],
                         start=False, stop=True).then_inc(s_s, 1)

            def batch(b, post, prep):
                pe.wait_ge(s_qk, b * 2 + 2)
                scores(b, 0)
                values()
                used = 0
                for n in range(TB):
                    i = ORDER[n]
                    pe.wait_ge(s_prob, b * TB + (n + 1))
                    first = used
                    for lo in range(0, i + 1, 4):
                        if used >= 2:
                            pe.wait_ge(s_probT, b * TURNS + (used - 1))
                        for j in range(lo, min(lo + 4, i + 1)):
                            m = t.transpose(turn[used % 2][:, (j - lo) * P:(j - lo + 1) * P],
                                            prob[:, n % 2, j * P:(j + 1) * P], ident[:])
                        m.then_inc(s_turn, 1)
                        used += 1
                    if n + 1 < TB:
                        scores(b, n + 1)
                    elif post:
                        logits(b - 1, [1])
                    if n == 0:
                        pe.wait_ge(s_v, b + 1)
                    if n >= 2:
                        pe.wait_ge(s_x2, b * TB + (n - 1))
                    for j in range(i + 1):
                        if j % 4 == 0:
                            pe.wait_ge(s_probT, b * TURNS + (first + j // 4 + 1))
                        m = t.matmul(summ[n % 2][:, 0:P], probT[:, n % 2, j, :], v[:, j, :],
                                     start=(j == 0), stop=(j == i))
                    m.then_inc(s_att, 1)
                    if n == 0 and prep:
                        turn_normed(b + 1)
                    if n == 1 and prep:
                        pe.wait_ge(s_xnT, b + 2)
                        project(0, 1)
                    if n == 3 and prep:
                        pe.wait_ge(s_rawc, b * 2 + 1)
                        project(2, 1)
                    if n == 4 and post:
                        if prep:
                            pe.wait_ge(s_rawc, b * 2 + 2)
                        turn_normed2(b - 1)
                    if n == 6 and post:
                        pe.wait_ge(s_hi2, b)
                        pe.wait_ge(s_lo2, b)
                        logits(b - 1, [0])
                if post:
                    pe.wait_ge(s_x2, b * TB + (TB - 1))
                    pe.wait_ge(s_lg, b)
                    turn_logits(b - 1)

            pe.wait_ge(s_ident, 1)
            turn_normed(0)
            pe.wait_ge(s_wvo, 32)
            t.transpose(turn[0][:, 0:P], wvo[:, 0, :], ident[:]).then_inc(s_pe0, 1)
            pe.wait_ge(s_xnT, 1)
            project(0, 0)
            project(1, 1)
            pe.wait_ge(s_act0, 2)
            t.matmul(turn[0][:, 0:P], wvo[:, 1, :], wvo[:, 2, :], start=True, stop=True).then_inc(s_pe0, 1)
            pe.wait_ge(s_rows, 5 * 16)
            t.transpose(turn[1][:, 0:NROWS], rows[:], ident[0:NROWS, 0:NROWS]).then_inc(s_pe0, 1)
            pe.wait_ge(s_w4, 1)
            pe.wait_ge(s_rot, 1)
            project(2, 0)
            pe.wait_ge(s_rot, 2)
            project(3, 1)
            pe.wait_ge(s_const, 6)
            pe.wait_ge(s_act0, 5)
            batch(0, False, True)
            with nc.tensor.Fori(1, B - 1) as b:
                batch(b, True, True)
            batch(B - 1, True, False)
            def split_products(out_ap, w, at, xs, first, last):
                for n, (ww, xx) in enumerate(((w_hi, xs[0]), (w_hi, xs[1]), (w_lo, xs[0]))):
                    m = t.matmul(out_ap, ww[:, w, at:at + P], xx, start=(first and n == 0), stop=(last and n == 2))
                return m

            def hidden(c, s, w, f, first=False):
                if not first:
                    pe.wait_ge(s_gelu, s * NF + (f + 1 - NF))
                at = bass.ds(c * CH, CH)
                split_products(hbank[f], w, f * P, (xT_hi[:, at], xT_lo[:, at]), True, True).then_inc(s_h, 1)

            def output(s, w, par, f):
                if f % 2 == 0:
                    pe.wait_ge(s_hilo, s * 2 + (f // 2 + 1))
                m = split_products(turn[par][:], w, F + f * P, (h_hi[:, par, f, :], h_lo[:, par, f, :]),
                                   f == 0, f == NF - 1)
                if f == NF - 1:
                    m.then_inc(s_y, 1)

            pe.wait_ge(s_wlo, 1)
            for f in range(NF):
                hidden(0, 0, 0, f, first=True)
            for f in range(NF):
                hidden(1, 1, 0, f)
            for i in range(TB):
                pe.wait_ge(s_xn2, (B - 1) * TB + (i + 1))
                m = t.transpose(summ[i // 4][:, (i % 4) * P:(i % 4 + 1) * P], xn2[:, i, :], ident[:])
                if i % 4 == 3:
                    m.then_inc(s_xn2p, 1)
            for f in range(NF):
                output(0, 0, 0, f)
            for c in range(2):
                pe.wait_ge(s_hi2, B + c)
                pe.wait_ge(s_lo2, B + c)
                at = slice((B - 1) * T + c * 512, (B - 1) * T + (c + 1) * 512)
                for n, (gg, xx) in enumerate(((gw_hi, xT_hi), (gw_hi, xT_lo), (gw_lo, xT_hi))):
                    m = t.matmul(summ[c][:], gg[:], xx[:, at], start=(n == 0), stop=(n == 2))
                m.then_inc(s_lgp, 1)
            for f in range(NF):
                hidden(2, 2, 0, f)
            pe.wait_ge(s_lg, B + 1)
            turn_logits(B - 1)
            for f in range(NF):
                output(1, 0, 1, f)

            def count(n):
                pe.wait_ge(s_cnt, n)
                t.matmul(summ[1][:, 0:1], ones_b[:], count_b[:], start=True, stop=True).then_inc(s_tot, 1)

            for f in range(NF):
                hidden(3, 3, 0, f)
            pe.wait_ge(s_gated, 1)
            for f in range(NF):
                output(2, 0, 0, f)

            def search(c, s, n, w, par, w_before, bits=BITS):
                for f in range(NF):
                    hidden(c, s, w, f)
                    if f % 2 and f // 2 < bits:
                        count(n + (f // 2 + 1))
                pe.wait_ge(s_gated, s - 2)
                for f in range(NF):
                    output(s - 1, w_before, 1 - par, f)
                    if f % 2 and f // 2 + 2 < bits:
                        count(n + (f // 2 + 3))

            with nc.tensor.Fori(0, (NC - LEAD) // 2) as r:
                for j in range(2):
                    s = r * 2 + (LEAD + j)
                    search(s, s, r * (2 * BITS) + j * BITS, 0, j, 0)

            pe.wait_ge(s_wlo, 2)
            for c in range(LATE):
                search(c, NC + c, BITS * (NC - LEAD + c), 1, c % 2, min(c, 1), BITS if c < LATE - 1 else LAST_BITS)
            for f in range(2):
                hidden(LATE, DIRECT, 1, f)
            count(NBIT + 1)
            pe.wait_ge(s_cnt, NBIT + 2)
            t.matmul(summ[0][:, 0:E * NT], before_b[:], eq_b[:], start=True, stop=True)
            t.matmul(summ[0][:, E * NT:2 * E * NT], ones_b[:], eq_b[:], start=True, stop=True).then_inc(s_tot, 1)
            for f in range(2, NF):
                hidden(LATE, DIRECT, 1, f)
            pe.wait_ge(s_gated, DIRECT - 2)
            for f in range(NF):
                output(DIRECT - 1, 1, 1, f)
            pe.wait_ge(s_gp, 1)
            for n in range(E * NT // P):
                m = t.transpose(summ[0][:, n * P:(n + 1) * P],
                                ra[:].rearrange("p e t -> p (e t)")[:, n * P:(n + 1) * P], ident[:])
            m.then_inc(s_gt, 1)
            for f in range(NF):
                hidden(LATE + 1, DIRECT + 1, 1, f)
            pe.wait_ge(s_gated, DIRECT - 1)
            for f in range(NF):
                output(DIRECT, 1, 0, f)
            for f in range(NF):
                hidden(LATE + 2, EARLY, 1, f)
            pe.wait_ge(s_gated, DIRECT)
            for f in range(NF):
                output(DIRECT + 1, 1, 1, f)
            for f in range(NF):
                hidden(LATE + 3, EARLY + 1, 1, f)
            pe.wait_ge(s_gated, DIRECT + 1)
            for f in range(NF):
                output(EARLY, 1, 0, f)

            def position(e, c, s, w, par, w_before):
                for f in range(NF):
                    hidden(c, s, w, f)
                for f in range(NF):
                    output(s - 1, w_before, 1 - par, f)

            def expert(e, w):
                pe.wait_ge(s_wlo, e + 1)
                position(e, 0, e * NC, w, 0, 1 - w)
                position(e, 1, e * NC + 1, w, 1, w)
                with nc.tensor.Fori(1, NC // 2) as cp:
                    for j in range(2):
                        position(e, cp * 2 + j, e * NC + (cp * 2 + j), w, j, w)

            expert(2, 0)
            with nc.tensor.Fori(1, E // 2 - 1) as ep:
                expert(ep * 2 + 1, 1)
                expert(ep * 2 + 2, 0)
            expert(E - 1, 1)

            def turn_into(bank, at):
                for i in range(CH // P):
                    m = t.transpose(summ[bank][:, i * P:(i + 1) * P], at[:, i * P:(i + 1) * P], ident[:])
                m.then_inc(s_fin, 1)

            def turn_result(c):
                pe.wait_ge(s_acc, 2 + NC * E + c + 1)
                turn_into(c % 2, outT[:, c * CH:(c + 1) * CH])

            pe.wait_ge(s_wlo, NE)
            for c in range(NC):
                position(E, c, E * NC + c, 0, c % 2, 1 if c == 0 else 0)
                if c >= 2:
                    turn_result(c - 2)
            pe.wait_ge(s_res, NC - 3)
            turn_into(0, outT[:, (NC - 1) * CH:])
            for f in range(NF):
                output(NE * NC - 1, 0, 1, f)
            pe.wait_ge(s_res, NC - 2)
            pe.wait_ge(s_acc, 2 + NC * E + NC - 1)
            turn_into(1, outT[:, (NC - 2) * CH:(NC - 1) * CH])
            pe.wait_ge(s_res, NC - 1)
            pe.wait_ge(s_gated, NE * NC)
            turn_into(0, gated[:, 1, :])

        @block.vector
        def _(dve):
            vec = nc.vector

            class Chain:

                def __init__(self, base):
                    self.base, self.n = base, 0

                def then(self, ins):
                    self.n += 1
                    ins.then_inc(s_dve, 1)
                    dve.wait_ge(s_dve, self.base + self.n)

            start = Chain(0)
            for n in range(NBIT):
                m = vec.memset(bit[:, n:n + 1], 1 << (NBIT - 1 - n))
            start.then(m)
            vec.memset(bit[:, NBIT:NBIT + 1], 0)
            start.then(vec.memset(cand[:], 1 << (NBIT - 1)))

            def tile_of(b, i):
                return x2[:, bass.ds(b * TB + i, 1), :].rearrange("p a d -> p (a d)")

            NEWTON = 3 + 3 * 3

            def inverse_root(out, var, n, chain):
                w, y, z = nw[:, 0, 0:n], nw[:, 1, 0:n], nw[:, 2, 0:n]
                chain.then(vec.tensor_scalar(w, var, EPS, None, ALU.add))
                chain.then(vec.tensor_scalar(nwi[:, 0:n], w.bitcast(I32), 1, None, ALU.logical_shift_right))
                chain.then(vec.tensor_scalar(y.bitcast(I32), nwi[:, 0:n], -1.0, float(RSQRT_MAGIC), ALU.mult, ALU.add))
                for r in range(3):
                    chain.then(vec.tensor_tensor(z, y, w, ALU.mult))
                    chain.then(vec.scalar_tensor_tensor(z, z, -0.5, y, ALU.mult, ALU.mult))
                    if r < 2:
                        chain.then(vec.scalar_tensor_tensor(y, z, 1.5, y, ALU.add, ALU.mult))
                return vec.scalar_tensor_tensor(out, z, 1.5, y, ALU.add, ALU.mult)

            def rotate(j, slot, n):
                dve.wait_ge(s_proj, n)
                vec.tensor_tensor((q_cos, q_sin, k_cos, k_sin)[j], big[slot][:], (costab, sintab)[j % 2],
                                  ALU.mult).then_inc(s_rot, 1)

            def add_key():
                vec.tensor_tensor(k, k_cos, k_sin, ALU.add).then_inc(s_qk, 1)

            def row_max(b, n):
                i = ORDER[n]
                dve.wait_ge(s_s, b * TB + (n + 1))
                vec.tensor_reduce(neg_max[:, i:i + 1], big[0][:, 0:(i + 1) * P], AX.X, ALU.max,
                                  negate=True).then_inc(s_max, 1)

            def statistics2(b, chain):
                for i in range(TB):
                    m = vec.bn_aggr(mv2[:, i, :], stats2[:, i, :])
                chain.then(m)
                chain.then(inverse_root(inv2[:], mv2[:, :, 1], TB, chain))

            def scale1(b):
                for i in range(TB):
                    vec.tensor_scalar(xn[:, i, :], tile_of(b, i), mv[:, bass.ds(b * TB + i, 1), 0],
                                      inv1[:, bass.ds(b * TB + i, 1)], ALU.subtract, ALU.mult).then_inc(s_xn, 1)

            def scale2(b):
                for i in range(TB):
                    vec.tensor_scalar(xn2[:, i, :], tile_of(b, i), mv2[:, i, 0:1], inv2[:, i:i + 1],
                                      ALU.subtract, ALU.mult).then_inc(s_xn2, 1)

            def low_part(b):
                dve.wait_ge(s_xn2p, b + 1)
                dve.wait_ge(s_hi2, b + 1)
                at = bass.ds(b * T, T)
                vec.tensor_tensor(xT_lo[:, at], big[1][:], xT_hi[:, at].bitcast(F32), ALU.subtract).then_inc(s_lo2, 1)

            def logits_by_token(b):
                dve.wait_ge(s_lgT, b + 1)
                vec.tensor_copy(lg[:, :, bass.ds(b * TB, TB)],
                                summ[0][:, 256:256 + TB * E].rearrange("p (t e) -> p e t", e=E)).then_inc(s_lgc, 1)

            def batch(b, post, prep, chain):
                row_max(b, 0)
                if prep:
                    dve.wait_ge(s_xnp, b + 1)
                    scale1(b + 1)
                for n in range(TB):
                    i = ORDER[n]
                    if n + 1 < TB:
                        row_max(b, n + 1)
                    if n == 0 and post:
                        statistics2(b - 1, chain)
                    if n == 1 and post:
                        scale2(b - 1)
                    if n == 5 and post:
                        low_part(b - 1)
                    if n == 7 and prep:
                        dve.wait_ge(s_s, b * TB + TB)
                        dve.wait_ge(s_rot, b * 2 + 6)
                        dve.wait_ge(s_sin, b * 2 + 2)
                        add_key()
                    if n:
                        dve.wait_ge(s_x2, b * TB + n)
                    dve.wait_ge(s_prob, b * TB + (n + 1))
                    chain.then(vec.reciprocal(row_inv[:, i:i + 1], row_sum[:, i:i + 1]))
                    dve.wait_ge(s_att, b * TB + (n + 1))
                    vec.scalar_tensor_tensor(tile_of(b, i), summ[n % 2][:, 0:P], row_inv[:, i:i + 1],
                                             tile_of(b, i), ALU.mult, ALU.add).then_inc(s_x2, 1)
                    if n:
                        vec.bn_stats(stats2[:, ORDER[n - 1], :], tile_of(b, ORDER[n - 1]))
                dve.wait_ge(s_x2, b * TB + TB)
                vec.memset(nothing_v[:], 0.0)
                chain.then(vec.bn_stats(stats2[:, ORDER[TB - 1], :], tile_of(b, ORDER[TB - 1])))
                vec.memset(nothing_v[:], 0.0)
                if post:
                    logits_by_token(b - 1)

            dve.wait_ge(s_x, 16)
            for i in range(TB):
                m = vec.bn_stats(stats[:, i, :], x2[:, i, :])
            start.then(m)
            for i in range(TB):
                m = vec.bn_aggr(mv[:, i, :], stats[:, i, :])
            start.then(m)
            start.then(inverse_root(inv1[:, 0:TB], mv[:, 0:TB, 1], TB, start))
            scale1(0)
            H = D // 2
            dve.wait_ge(s_wqk, 32)
            vec.tensor_copy(w4[:, 2, :], wqk[:, 1, :])
            vec.tensor_copy(w4[:, 3, 0:H], wqk[:, 1, H:D])
            vec.tensor_copy(w4[:, 3, H:D], wqk[:, 1, 0:H]).then_inc(s_w4, 1)
            dve.wait_ge(s_xr, 16)
            for i in range(TB, NT):
                m = vec.bn_stats(stats[:, i, :], x2[:, i, :])
            start.then(m)
            dve.wait_ge(s_trig, 32)
            for j in range(4):
                rotate(j, j % 2, j + 1)
                for i in range(TB * (j + 1), min(TB * (j + 2), NT)):
                    m = vec.bn_aggr(mv[:, i, :], stats[:, i, :])
            dve.wait_ge(s_rot, 4)
            add_key()
            start.then(m)
            dve.wait_ge(s_act0, 5)
            vec.tensor_tensor(gw_lo[:, 0:E], cols[:, ROWS_GW:NROWS], gw_hi[:, 0:E].bitcast(F32),
                              ALU.subtract).then_inc(s_gw, 1)
            m = inverse_root(inv1[:, TB:NT], mv[:, TB:NT, 1], NT - TB, start)
            start.then(m)
            batch(0, False, True, start)
            LINKS = 1 + NEWTON + TB + 1
            first = start.n
            with nc.vector.Fori(1, B - 1) as b:
                chain = Chain((b - 1) * LINKS + first)
                batch(b, True, True, chain)
                assert chain.n == LINKS, chain.n
            chain = Chain(first + LINKS * (B - 2))
            batch(B - 1, True, False, chain)
            statistics2(B - 1, chain)
            scale2(B - 1)
            for c in range(2):
                dve.wait_ge(s_xn2p, B + c)
                dve.wait_ge(s_hi2, B + c)
                at = slice((B - 1) * T + c * 512, (B - 1) * T + (c + 1) * 512)
                vec.tensor_tensor(xT_lo[:, at], summ[c][:], xT_hi[:, at].bitcast(F32), ALU.subtract).then_inc(s_lo2, 1)

            base = chain.base + chain.n

            def hi_part(s, par, half):
                dve.wait_ge(s_gelu, s * NF + (2 * half + 2))
                fs = slice(2 * half, 2 * half + 2)
                vec.tensor_copy(h_hi[:, par, fs, :], h[par][:, fs, :]).then_inc(s_hp, 1)

            def lo_part(s, par, half):
                dve.wait_ge(s_hp, s * 2 + (half + 1 - 2 * EARLY))
                fs = slice(2 * half, 2 * half + 2)
                vec.tensor_tensor(h_lo[:, par, fs, :], h[par][:, fs, :], h_hi[:, par, fs, :].bitcast(F32),
                                  ALU.subtract).then_inc(s_hilo, 1)

            def add_bias(s, par):
                dve.wait_ge(s_y, s + 1)
                dve.wait_ge(s_acc, s + 1)
                vec.tensor_scalar(gated[:, par, :], turn[par][:], cols[:, ROWS_B2:ROWS_B2 + 1], None,
                                  ALU.add).then_inc(s_gated, 1)

            def gate(s, e, c, par, n_loads, added=None):
                dve.wait_ge(s_gbc, n_loads * 16)
                dve.wait_ge(s_y, s + 1)
                dve.wait_ge(s_acc, s + 1 if added is None else added)
                vec.scalar_tensor_tensor(gated[:, par, :], turn[par][:], cols[:, bass.ds(ROWS_B2 + e, 1)],
                                         gate_bc[:, bass.ds(c * CH, CH)], ALU.add, ALU.mult).then_inc(s_gated, 1)

            def keep(c):
                dve.wait_ge(s_y, NC + c + 1)
                vec.tensor_scalar(late[:, c, :], turn[c % 2][:], cols[:, ROWS_B2 + 1:ROWS_B2 + 2], None,
                                  ALU.add).then_inc(s_gated, 1)

            chain = Chain(base)
            add_bias(0, 0)
            dve.wait_ge(s_whi, 2)
            dve.wait_ge(s_wlo, 1)
            vec.tensor_tensor(w_lo[:, 1, :], w_raw[:, 1, :], w_hi[:, 1, :].bitcast(F32),
                              ALU.subtract).then_inc(s_wlo, 1)
            logits_by_token(B - 1)
            dve.wait_ge(s_lgc, B)
            by_token = "p e t -> p t e"

            def spread(v_):
                return v_.unsqueeze(1).to_broadcast([P, E, NT])

            chain.then(vec.tensor_reduce(rs[:, 0, :], lg[:].rearrange(by_token), AX.X, ALU.max))
            chain.then(vec.tensor_tensor(ra[:], lg[:], spread(rs[:, 0, :]), ALU.subtract))
            chain.then(vec.tensor_scalar(ra[:], ra[:], -100.0, None, ALU.max))
            chain.then(vec.tensor_scalar(rb[:], ra[:], LOG2E, ROUND, ALU.mult, ALU.add))
            chain.then(vec.tensor_scalar(rb[:], rb[:], ROUND, -127.0, ALU.subtract, ALU.max))
            chain.then(vec.tensor_scalar(pow2[:], rb[:], 127.0, 8388608.0, ALU.add, ALU.mult))
            chain.then(vec.scalar_tensor_tensor(ra[:], rb[:], -LN2_HI, ra[:], ALU.mult, ALU.add))
            chain.then(vec.scalar_tensor_tensor(ra[:], rb[:], -LN2_LO, ra[:], ALU.mult, ALU.add))
            fact = [1.0, 1.0, 2.0, 6.0, 24.0, 120.0, 720.0, 5040.0]
            add_bias(1, 1)
            chain.then(vec.tensor_scalar(rb[:], ra[:], 1.0 / fact[7], None, ALU.mult))
            for d in range(6, 0, -1):
                chain.then(vec.scalar_tensor_tensor(rb[:], rb[:], 1.0 / fact[d], ra[:], ALU.add, ALU.mult))
            chain.then(vec.scalar_tensor_tensor(rb[:], rb[:], 1.0, pow2[:].bitcast(F32), ALU.add, ALU.mult))
            chain.then(vec.tensor_reduce(rs[:, 0, :], rb[:].rearrange(by_token), AX.X, ALU.add))
            chain.then(vec.reciprocal(rs[:, 1, :], rs[:, 0, :]))
            chain.then(vec.tensor_tensor(lg[:], rb[:], spread(rs[:, 1, :]), ALU.mult))
            flat = "p e t -> p (e t)"
            scores, ra_ = lg[:].rearrange(flat), ra[:].rearrange(flat)

            def search(s, n0, par, chain, bits=BITS, kept=None):
                for n in range(bits):
                    vec.tensor_scalar(ra_, scores, cand[:].bitcast(F32), None, ALU.is_ge, ALU.add,
                                      accum_out=count_b[:]).then_inc(s_cnt, 1)
                    vec.tensor_tensor(cand_next[:], cand[:], bit[:, bass.ds(n0 + (n + 1), 1)], ALU.bitwise_or)
                    if n == 1 and kept is not None:
                        keep(kept)
                    elif n == 1:
                        add_bias(s - 2, par)
                    dve.wait_ge(s_tot, n0 + (n + 1))
                    chain.then(vec.tensor_scalar(flag[:], summ[1][:, 0:1], float(K_TOP), bit[:, bass.ds(n0 + n, 1)],
                                                 ALU.is_lt, ALU.mult))
                    chain.then(vec.tensor_tensor(cand[:], cand_next[:], flag[:], ALU.bitwise_xor))

            base += chain.n
            with nc.vector.Fori(0, (NC - LEAD) // 2) as r:
                chain = Chain(r * (4 * BITS) + base)
                for j in range(2):
                    search(r * 2 + (LEAD + j), r * (2 * BITS) + j * BITS, j, chain)
                assert chain.n == 4 * BITS
            chain = Chain(base + 2 * BITS * (NC - LEAD))
            for c in range(LATE):
                search(NC + c, BITS * (NC - LEAD + c), c % 2, chain, BITS if c < LATE - 1 else LAST_BITS,
                       c - 2 if c >= 2 else None)
            limit = cand[:].bitcast(F32)
            vec.tensor_scalar(ra_, scores, limit, None, ALU.is_gt, ALU.add, accum_out=count_b[:]).then_inc(s_cnt, 1)
            vec.tensor_scalar(eq_b[:], scores, limit, None, ALU.is_equal).then_inc(s_cnt, 1)
            keep(LATE - 2)
            dve.wait_ge(s_tot, NBIT + 2)
            before, inside = summ[0][:, 0:E * NT], summ[0][:, E * NT:2 * E * NT]
            chain.then(vec.tensor_tensor_scan(ra_, inside, zeros[:], 0.0, ALU.add, ALU.add))
            chain.then(vec.tensor_tensor(ra_, ra_, inside, ALU.subtract))
            chain.then(vec.tensor_tensor(ra_, ra_, before, ALU.add))
            chain.then(vec.tensor_copy(count_f[:, 0:1], summ[1][:, 0:1]))
            chain.then(vec.tensor_scalar(ra_, ra_, count_f[:, 0:1], float(K_TOP), ALU.add, ALU.is_lt))
            chain.then(vec.tensor_tensor(ra_, ra_, eq_b[:], ALU.mult))
            chain.then(vec.scalar_tensor_tensor(ra_, scores, limit, ra_, ALU.is_gt, ALU.add))
            vec.tensor_tensor(ra_, ra_, scores, ALU.mult).then_inc(s_gp, 1)
            dve.wait_ge(s_gt, 1)
            vec.tensor_copy(g_rows[:].rearrange("p n c -> p (n c)"), summ[0][:, 0:E * NT]).then_inc(s_gTc, 1)
            keep(LATE - 1)

            def split_hidden(s, par):
                for half in range(2):
                    hi_part(s, par, half)
                    lo_part(s, par, half)

            dve.wait_ge(s_hilo, 2 * EARLY)
            split_hidden(EARLY, 0)
            gate(DIRECT, 1, LATE, 0, 1, added=2 + NC)
            gate(DIRECT + 1, 1, LATE + 1, 1, 1, added=2 + NC)
            split_hidden(EARLY + 1, 1)
            gate(EARLY, 1, LATE + 2, 0, 2, added=3 + NC)

            def add_result(c, par, n_fin=None):
                dve.wait_ge(s_fin, c + 1 if n_fin is None else n_fin)
                o = x2[:, bass.ds(c * (CH // P), CH // P), :].rearrange("p t d -> p (t d)")
                vec.tensor_tensor(o, o, summ[par][:], ALU.add).then_inc(s_res, 1)

            def expert(e, last=False):
                split_hidden(e * NC, 0)
                gate(e * NC - 1, e - 1, NC - 1, 1, (e - 1) * 4)
                split_hidden(e * NC + 1, 1)
                gate(e * NC, e, 0, 0, (e - 1) * 4 + 1)
                with nc.vector.Fori(1, NC // 2) as cp:
                    split_hidden(e * NC + (cp * 2), 0)
                    gate(e * NC + (cp * 2 - 1), e, cp * 2 - 1, 1, (e - 1) * 4 + cp)
                    if last:
                        add_result(cp * 2 - 2, 0)
                    split_hidden(e * NC + (cp * 2 + 1), 1)
                    gate(e * NC + (cp * 2), e, cp * 2, 0, (e - 1) * 4 + (cp + 1))
                    if last:
                        add_result(cp * 2 - 1, 1)

            expert(2)
            with nc.vector.Fori(1, E // 2 - 1) as ep:
                expert(ep * 2 + 1)
                expert(ep * 2 + 2)
            expert(E - 1)
            expert(E, last=True)
            add_result(NC - 1, 0, NC - 1)
            gate(NE * NC - 1, E, NC - 1, 1, E * 4)
            add_result(NC - 2, 1, NC)
            dve.wait_ge(s_res, NC - 1)
            add_result(NC - 1, 0, NC + 1)


def rotation_tables(T, D, base=10000.0):
    import numpy as np
    half = D // 2
    freqs = np.power(np.float32(base), -np.arange(half, dtype=np.float32) / np.float32(half)).astype(np.float32)
    angles = (freqs[:, None] * np.arange(T, dtype=np.float32)[None, :]).astype(np.float32)
    cos, sin = np.cos(angles).astype(np.float32), np.sin(angles).astype(np.float32)
    return np.concatenate([cos, cos]), np.concatenate([-sin, sin])


_INS = ['L0_attn_x', 'L0_attn_wq', 'L0_attn_wk', 'L0_attn_wv', 'L0_attn_wo', 'L0_ffn_gate_weight', 'L0_ffn_W1',
        'L0_ffn_b1', 'L0_ffn_W2', 'L0_ffn_b2', 'L0_ffn_Ws1', 'L0_ffn_bs1', 'L0_ffn_Ws2', 'L0_ffn_bs2']


def kernel(**inputs):
    import numpy as np
    import concourse.bacc as bacc
    from concourse.bass_utils import run_bass_kernel_spmd

    nc = bacc.Bacc("TRN2", target_bir_lowering=False, num_devices=1)
    arrays = {name: np.ascontiguousarray(inputs[name]) for name in _INS}
    B, T, D = arrays['L0_attn_x'].shape
    arrays['cos'], arrays['sin'] = rotation_tables(T, D)
    args = [nc.dram_tensor(name, a.shape, mybir.dt.from_np(a.dtype), kind="ExternalInput").ap()
            for name, a in arrays.items()]
    args.append(nc.dram_tensor("out", (B, T, D), F32, kind="ExternalOutput").ap())
    E = arrays['L0_ffn_gate_weight'].shape[0]
    args.append(nc.dram_tensor("gate_rows", (E, B * T), F32, kind="Internal").ap())
    moe_layer(nc, *args)
    r = run_bass_kernel_spmd(nc, [arrays], core_ids=[0])
    return r.results[0]["out"]
```
